# Optimizing a Trainium2 kernel written in Bass

```python
import numpy as np
import jax
import jax.numpy as jnp

def _softmax(x, axis=-1):
    return jax.nn.softmax(x, axis=axis)

def _gelu(x):
    return jax.nn.gelu(x, approximate=True)

def _silu(x):
    return jax.nn.silu(x)

def _sigmoid(x):
    return jax.nn.sigmoid(x)

def _layernorm(x, axis=-1, eps=1e-05):
    m = jnp.mean(x, axis=axis, keepdims=True)
    v = jnp.var(x, axis=axis, keepdims=True)
    return (x - m) / jnp.sqrt(v + eps)

def _scatter_add(tgt, idx, src, axis=0):
    return tgt.at[idx].add(src)

def _segment_sum(src, seg, n):
    return jax.ops.segment_sum(src, seg, n)
kernel_name = 'mk_seq_postln_d1_jaxref_r4_b829c3'

def setup_inputs(seed: int=0):
    np.random.seed(seed)
    _w = jnp.asarray

    def _L0_attn_setup():
        import jax, jax.numpy as jnp
        import numpy as np
        B, N, D = (2, 1024, 256)
        DS = 256
        H = 1024
        EPS = 1e-05

        def _layernorm(x, w, b):
            mu = jnp.mean(x, axis=-1, keepdims=True)
            var = jnp.mean((x - mu) ** 2, axis=-1, keepdims=True)
            return (x - mu) * jax.lax.rsqrt(var + EPS) * w + b

        def _selective_scan(deltaA, deltaB_u):

            def step(h, inp):
                dA, dBu = inp
                h = dA * h + dBu
                return (h, h)
            h0 = jnp.zeros((deltaB_u.shape[0], deltaB_u.shape[2]), deltaB_u.dtype)
            _, ys = jax.lax.scan(step, h0, (jnp.swapaxes(deltaA, 0, 1), jnp.swapaxes(deltaB_u, 0, 1)))
            return jnp.swapaxes(ys, 0, 1)

        def _forward(x, norm1_w, norm1_b, gate_w, gate_b, state_w, state_b, out_w, out_b, norm2_w, norm2_b, mlp_w1, mlp_b1, mlp_w2, mlp_b2):
            xn = _layernorm(x, norm1_w, norm1_b)
            g = xn @ gate_w + gate_b
            gate, gate_gate = jnp.split(g, 2, axis=-1)
            gate = jax.nn.silu(gate)
            gate_gate = jax.nn.silu(gate_gate)
            u = xn * gate @ state_w + state_b
            Bm = gate_gate @ state_w + state_b
            delta = jax.nn.softplus(jnp.mean(xn @ state_w + state_b, axis=-1, keepdims=True))
            deltaA = jnp.exp(-delta)
            deltaB_u = delta * Bm * u
            y = _selective_scan(deltaA, deltaB_u)
            ssm_out = y @ out_w + out_b
            x = x + ssm_out
            x2 = _layernorm(x, norm2_w, norm2_b)
            mlp = jax.nn.gelu(x2 @ mlp_w1 + mlp_b1, approximate=False) @ mlp_w2 + mlp_b2
            return x + mlp
        key = jax.random.key(seed)
        ks = jax.random.split(key, 12)
        s = 0.02
        p = lambda k, shape: jax.random.normal(k, shape, jnp.float32) * s
        return {'x': jax.random.normal(ks[0], (B, N, D), jnp.float32), 'norm1_w': jnp.ones((D,), jnp.float32), 'norm1_b': jnp.zeros((D,), jnp.float32), 'gate_w': p(ks[1], (D, 2 * D)), 'gate_b': p(ks[2], (2 * D,)), 'state_w': p(ks[3], (D, DS)), 'state_b': p(ks[4], (DS,)), 'out_w': p(ks[5], (DS, D)), 'out_b': p(ks[6], (D,)), 'norm2_w': jnp.ones((D,), jnp.float32), 'norm2_b': jnp.zeros((D,), jnp.float32), 'mlp_w1': p(ks[7], (D, H)), 'mlp_b1': p(ks[8], (H,)), 'mlp_w2': p(ks[9], (H, D)), 'mlp_b2': p(ks[10], (D,))}
    _L0_attn_in = _L0_attn_setup()

    def _L0_ffn_setup():
        import jax, jax.numpy as jnp
        import numpy as np
        from jax.scipy.linalg import expm
        B, S, D, E, K, NROT = (2, 512, 256, 8, 2, 3)
        EPS = 1e-05

        def _gelu(x):
            return jax.nn.gelu(x, approximate=False)

        def _forward(x, ln_gamma, ln_beta, abel_w, abel_b, moe_gate_w, moe_gate_b, ew1, eb1, ew2, eb2, gens, gc_w, gc_b):
            residual = x
            mu = jnp.mean(x, axis=-1, keepdims=True)
            var = jnp.mean((x - mu) ** 2, axis=-1, keepdims=True)
            xn = (x - mu) * jax.lax.rsqrt(var + EPS) * ln_gamma + ln_beta
            abel_out = _gelu(xn @ abel_w + abel_b)
            logits = xn @ moe_gate_w + moe_gate_b
            topw, topi = jax.lax.top_k(logits, K)
            topw = jax.nn.softmax(topw, axis=-1)
            w_dense = jnp.sum(jax.nn.one_hot(topi, E, dtype=xn.dtype) * topw[..., None], axis=-2)
            h = _gelu(jnp.einsum('bsd,edh->ebsh', xn, ew1) + eb1[:, None, None, :])
            eo = jnp.einsum('ebsh,ehd->ebsd', h, ew2) + eb2[:, None, None, :]
            moe_out = jnp.einsum('ebsd,bse->bsd', eo, w_dense)
            for i in range(NROT):
                moe_out = moe_out @ expm(gens[i])
            combined = jnp.concatenate([abel_out, moe_out], axis=-1)
            gate = jax.nn.sigmoid(combined @ gc_w + gc_b)
            mixed = abel_out * (1.0 - gate) + moe_out * gate
            return residual + mixed
        key = jax.random.key(seed)
        ks = jax.random.split(key, 16)
        sc = 0.02
        x = jax.random.normal(ks[0], (B, S, D), jnp.float32)
        ln_gamma = 1.0 + sc * jax.random.normal(ks[1], (D,), jnp.float32)
        ln_beta = sc * jax.random.normal(ks[2], (D,), jnp.float32)
        abel_w = sc * jax.random.normal(ks[3], (D, D), jnp.float32)
        abel_b = sc * jax.random.normal(ks[4], (D,), jnp.float32)
        moe_gate_w = sc * jax.random.normal(ks[5], (D, E), jnp.float32)
        moe_gate_b = sc * jax.random.normal(ks[6], (E,), jnp.float32)
        ew1 = sc * jax.random.normal(ks[7], (E, D, 2 * D), jnp.float32)
        eb1 = sc * jax.random.normal(ks[8], (E, 2 * D), jnp.float32)
        ew2 = sc * jax.random.normal(ks[9], (E, 2 * D, D), jnp.float32)
        eb2 = sc * jax.random.normal(ks[10], (E, D), jnp.float32)
        g = sc * jax.random.normal(ks[11], (NROT, D, D), jnp.float32)
        gens = 0.5 * (g - jnp.swapaxes(g, -1, -2))
        gc_w = sc * jax.random.normal(ks[12], (2 * D, 1), jnp.float32)
        gc_b = sc * jax.random.normal(ks[13], (1,), jnp.float32)
        return dict(x=x, ln_gamma=ln_gamma, ln_beta=ln_beta, abel_w=abel_w, abel_b=abel_b, moe_gate_w=moe_gate_w, moe_gate_b=moe_gate_b, ew1=ew1, eb1=eb1, ew2=ew2, eb2=eb2, gens=gens, gc_w=gc_w, gc_b=gc_b)
    _L0_ffn_in = _L0_ffn_setup()
    _d = {'L0_attn_x': _L0_attn_in['x'], 'L0_attn_norm1_w': _L0_attn_in['norm1_w'], 'L0_attn_norm1_b': _L0_attn_in['norm1_b'], 'L0_attn_gate_w': _L0_attn_in['gate_w'], 'L0_attn_gate_b': _L0_attn_in['gate_b'], 'L0_attn_state_w': _L0_attn_in['state_w'], 'L0_attn_state_b': _L0_attn_in['state_b'], 'L0_attn_out_w': _L0_attn_in['out_w'], 'L0_attn_out_b': _L0_attn_in['out_b'], 'L0_attn_norm2_w': _L0_attn_in['norm2_w'], 'L0_attn_norm2_b': _L0_attn_in['norm2_b'], 'L0_attn_mlp_w1': _L0_attn_in['mlp_w1'], 'L0_attn_mlp_b1': _L0_attn_in['mlp_b1'], 'L0_attn_mlp_w2': _L0_attn_in['mlp_w2'], 'L0_attn_mlp_b2': _L0_attn_in['mlp_b2'], 'L0_ffn_ln_gamma': _L0_ffn_in['ln_gamma'], 'L0_ffn_ln_beta': _L0_ffn_in['ln_beta'], 'L0_ffn_abel_w': _L0_ffn_in['abel_w'], 'L0_ffn_abel_b': _L0_ffn_in['abel_b'], 'L0_ffn_moe_gate_w': _L0_ffn_in['moe_gate_w'], 'L0_ffn_moe_gate_b': _L0_ffn_in['moe_gate_b'], 'L0_ffn_ew1': _L0_ffn_in['ew1'], 'L0_ffn_eb1': _L0_ffn_in['eb1'], 'L0_ffn_ew2': _L0_ffn_in['ew2'], 'L0_ffn_eb2': _L0_ffn_in['eb2'], 'L0_ffn_gens': _L0_ffn_in['gens'], 'L0_ffn_gc_w': _L0_ffn_in['gc_w'], 'L0_ffn_gc_b': _L0_ffn_in['gc_b']}
    _x0 = _d['L0_attn_x']
    _d['L0_attn_x'] = jax.random.normal(jax.random.fold_in(jax.random.key(seed), 1), (8, 512, 256), dtype=_x0.dtype)
    del _x0
    return _d

def reference(L0_attn_x, L0_attn_norm1_w, L0_attn_norm1_b, L0_attn_gate_w, L0_attn_gate_b, L0_attn_state_w, L0_attn_state_b, L0_attn_out_w, L0_attn_out_b, L0_attn_norm2_w, L0_attn_norm2_b, L0_attn_mlp_w1, L0_attn_mlp_b1, L0_attn_mlp_w2, L0_attn_mlp_b2, L0_ffn_ln_gamma, L0_ffn_ln_beta, L0_ffn_abel_w, L0_ffn_abel_b, L0_ffn_moe_gate_w, L0_ffn_moe_gate_b, L0_ffn_ew1, L0_ffn_eb1, L0_ffn_ew2, L0_ffn_eb2, L0_ffn_gens, L0_ffn_gc_w, L0_ffn_gc_b):

    def _L0_attn_ref(x, norm1_w, norm1_b, gate_w, gate_b, state_w, state_b, out_w, out_b, norm2_w, norm2_b, mlp_w1, mlp_b1, mlp_w2, mlp_b2):
        import jax, jax.numpy as jnp
        import numpy as np
        B, N, D = (2, 1024, 256)
        DS = 256
        H = 1024
        EPS = 1e-05

        def _layernorm(x, w, b):
            mu = jnp.mean(x, axis=-1, keepdims=True)
            var = jnp.mean((x - mu) ** 2, axis=-1, keepdims=True)
            return (x - mu) * jax.lax.rsqrt(var + EPS) * w + b

        def _selective_scan(deltaA, deltaB_u):

            def step(h, inp):
                dA, dBu = inp
                h = dA * h + dBu
                return (h, h)
            h0 = jnp.zeros((deltaB_u.shape[0], deltaB_u.shape[2]), deltaB_u.dtype)
            _, ys = jax.lax.scan(step, h0, (jnp.swapaxes(deltaA, 0, 1), jnp.swapaxes(deltaB_u, 0, 1)))
            return jnp.swapaxes(ys, 0, 1)

        def _forward(x, norm1_w, norm1_b, gate_w, gate_b, state_w, state_b, out_w, out_b, norm2_w, norm2_b, mlp_w1, mlp_b1, mlp_w2, mlp_b2):
            xn = _layernorm(x, norm1_w, norm1_b)
            g = xn @ gate_w + gate_b
            gate, gate_gate = jnp.split(g, 2, axis=-1)
            gate = jax.nn.silu(gate)
            gate_gate = jax.nn.silu(gate_gate)
            u = xn * gate @ state_w + state_b
            Bm = gate_gate @ state_w + state_b
            delta = jax.nn.softplus(jnp.mean(xn @ state_w + state_b, axis=-1, keepdims=True))
            deltaA = jnp.exp(-delta)
            deltaB_u = delta * Bm * u
            y = _selective_scan(deltaA, deltaB_u)
            ssm_out = y @ out_w + out_b
            x = x + ssm_out
            x2 = _layernorm(x, norm2_w, norm2_b)
            mlp = jax.nn.gelu(x2 @ mlp_w1 + mlp_b1, approximate=False) @ mlp_w2 + mlp_b2
            return x + mlp
        return _forward(x, norm1_w, norm1_b, gate_w, gate_b, state_w, state_b, out_w, out_b, norm2_w, norm2_b, mlp_w1, mlp_b1, mlp_w2, mlp_b2)

    def _L0_ffn_ref(x, ln_gamma, ln_beta, abel_w, abel_b, moe_gate_w, moe_gate_b, ew1, eb1, ew2, eb2, gens, gc_w, gc_b):
        import jax, jax.numpy as jnp
        import numpy as np
        from jax.scipy.linalg import expm
        B, S, D, E, K, NROT = (2, 512, 256, 8, 2, 3)
        EPS = 1e-05

        def _gelu(x):
            return jax.nn.gelu(x, approximate=False)

        def _forward(x, ln_gamma, ln_beta, abel_w, abel_b, moe_gate_w, moe_gate_b, ew1, eb1, ew2, eb2, gens, gc_w, gc_b):
            residual = x
            mu = jnp.mean(x, axis=-1, keepdims=True)
            var = jnp.mean((x - mu) ** 2, axis=-1, keepdims=True)
            xn = (x - mu) * jax.lax.rsqrt(var + EPS) * ln_gamma + ln_beta
            abel_out = _gelu(xn @ abel_w + abel_b)
            logits = xn @ moe_gate_w + moe_gate_b
            topw, topi = jax.lax.top_k(logits, K)
            topw = jax.nn.softmax(topw, axis=-1)
            w_dense = jnp.sum(jax.nn.one_hot(topi, E, dtype=xn.dtype) * topw[..., None], axis=-2)
            h = _gelu(jnp.einsum('bsd,edh->ebsh', xn, ew1) + eb1[:, None, None, :])
            eo = jnp.einsum('ebsh,ehd->ebsd', h, ew2) + eb2[:, None, None, :]
            moe_out = jnp.einsum('ebsd,bse->bsd', eo, w_dense)
            for i in range(NROT):
                moe_out = moe_out @ expm(gens[i])
            combined = jnp.concatenate([abel_out, moe_out], axis=-1)
            gate = jax.nn.sigmoid(combined @ gc_w + gc_b)
            mixed = abel_out * (1.0 - gate) + moe_out * gate
            return residual + mixed
        return _forward(x, ln_gamma, ln_beta, abel_w, abel_b, moe_gate_w, moe_gate_b, ew1, eb1, ew2, eb2, gens, gc_w, gc_b)
    x = L0_attn_x
    x = _layernorm(x + _L0_attn_ref(x, L0_attn_norm1_w, L0_attn_norm1_b, L0_attn_gate_w, L0_attn_gate_b, L0_attn_state_w, L0_attn_state_b, L0_attn_out_w, L0_attn_out_b, L0_attn_norm2_w, L0_attn_norm2_b, L0_attn_mlp_w1, L0_attn_mlp_b1, L0_attn_mlp_w2, L0_attn_mlp_b2), axis=-1)
    x = _layernorm(x + _L0_ffn_ref(x, L0_ffn_ln_gamma, L0_ffn_ln_beta, L0_ffn_abel_w, L0_ffn_abel_b, L0_ffn_moe_gate_w, L0_ffn_moe_gate_b, L0_ffn_ew1, L0_ffn_eb1, L0_ffn_ew2, L0_ffn_eb2, L0_ffn_gens, L0_ffn_gc_w, L0_ffn_gc_b), axis=-1)
    return x

_drawn_inputs = setup_inputs


def setup_inputs(seed=0):
    import zlib

    import numpy as np

    out = dict(_drawn_inputs(seed))
    spreads = {'L0_attn_norm1_w': (1.0, 0.6),
     'L0_attn_norm1_b': (0.0, 0.8),
     'L0_attn_norm2_w': (1.0, 0.6),
     'L0_attn_norm2_b': (0.0, 2.0)}
    factors = {'L0_attn_gate_w': 8.0,
     'L0_attn_gate_b': 8.0,
     'L0_attn_state_w': 8.0,
     'L0_attn_state_b': 8.0,
     'L0_attn_out_w': 8.0,
     'L0_attn_out_b': 42.88,
     'L0_attn_mlp_b1': 64.0,
     'L0_attn_mlp_b2': 43.248,
     'L0_ffn_ln_gamma': 8.0,
     'L0_ffn_ln_beta': 8.0,
     'L0_ffn_abel_b': 8.0,
     'L0_ffn_moe_gate_w': 4.405,
     'L0_ffn_moe_gate_b': 8.0,
     'L0_ffn_ew1': 4.137,
     'L0_ffn_eb1': 8.0,
     'L0_ffn_ew2': 4.022,
     'L0_ffn_eb2': 33.488,
     'L0_ffn_gens': 8.0,
     'L0_ffn_gc_w': 8.0,
     'L0_attn_mlp_w1': 4.143,
     'L0_attn_mlp_w2': 4.326}
    for name, (base, spread) in spreads.items():
        noise = np.random.default_rng([zlib.crc32(name.encode()), seed]).standard_normal(out[name].shape)
        drawn = base * np.exp(spread * noise) if base else spread * noise
        out[name] = jnp.asarray(drawn.astype(out[name].dtype))
    for name, factor in factors.items():
        out[name] = (out[name] * factor).astype(out[name].dtype)
    return out
```

```python
import concourse.bass as bass
from concourse import mybir
from contextlib import ExitStack


F32 = mybir.dt.float32
BF16 = mybir.dt.bfloat16
I32 = mybir.dt.int32
U32 = mybir.dt.uint32
ALU = mybir.AluOpType
ACT = mybir.ActivationFunctionType
AX = mybir.AxisListType

P = 128
BATCHES, TOKENS, D = 8, 512, 256
KC = D // P
TT = TOKENS // P
HID = 1024
HC = HID // P
EPS = 1e-5


def wait(eng, sem, value):
    if not isinstance(value, int) or value > 0:
        eng.wait_ge(sem, value)


def split_product(nc, dst, lhs, rhs, terms, start=True, stop=True):
    n, last = 0, None
    total = 3 * terms
    for k in range(terms):
        for a, b in ((0, 0), (0, 1), (1, 0)):
            last = nc.tensor.matmul(dst, lhs(a, k), rhs(b, k), start=start and n == 0,
                                    stop=stop and n == total - 1)
            n += 1
    return last



def mamba_half(nc, t, xp_dram):
    ctx = ExitStack()
    with ctx:
        def sb(name, shape, dt=F32):
            return ctx.enter_context(nc.sbuf_tensor(name, shape, dt))

        def pb(name, shape, dt=F32):
            return ctx.enter_context(nc.psum_tensor(name, shape, dt))

        def sem(name):
            return ctx.enter_context(nc.semaphore(name))

        ident = sb("ident", [P, P])
        neg_half = sb("neg_half", [P, TT])
        eps_t = sb("eps_t", [P, TT])
        n1w, n1b = sb("n1w", [P, KC]), sb("n1b", [P, KC])
        n2w, n2b = sb("n2w", [P, KC]), sb("n2b", [P, KC])
        gate_b = sb("gate_b", [P, 2 * KC])
        state_b = sb("state_b", [P, KC])
        mlp_b1 = sb("mlp_b1", [P, HC])
        out_b_row = sb("out_b_row", [P, D])
        mlp_b2_row = sb("mlp_b2_row", [P, D])
        state_b_row = sb("state_b_row", [P, D])
        vectors = [(n1w, "n1w"), (n1b, "n1b"), (n2w, "n2w"), (n2b, "n2b"), (gate_b, "gate_b"),
                   (state_b, "state_b"), (mlp_b1, "mlp_b1"), (out_b_row, "out_b_row"),
                   (mlp_b2_row, "mlp_b2_row"), (state_b_row, "state_b_row")]
        gate_w = sb("gate_w", [P, 2, KC, 2 * D], BF16)
        state_w = sb("state_w", [P, 2, KC, D], BF16)
        mean_w = sb("mean_w", [P, 2, KC, P], BF16)
        out_w = sb("out_w", [P, 2, KC, D], BF16)
        mlp_w1 = sb("mlp_w1", [P, 2, KC, HID], BF16)
        mlp_w2 = sb("mlp_w2", [P, 2, HC, D], BF16)
        weights = [(gate_w, "gate_w", KC, 2 * D), (state_w, "state_w", KC, D), (out_w, "out_w", KC, D),
                   (mlp_w1, "mlp_w1", KC, HID), (mlp_w2, "mlp_w2", HC, D)]
        staged = sb("staged", [P, 2, 2048])
        mean_col = sb("mean_col", [P, KC])
        mean_full = sb("mean_full", [P, KC, P])
        mean_b = sb("mean_b", [P, 1])

        x_in = sb("x_in", [P, 2, TT, D])
        x_ob = sb("x_ob", [P, TT, D])
        x_b2 = sb("x_b2", [P, TT, D])
        x_res = sb("x_res", [P, TT, D])
        st1, mv1, rs1 = sb("st1", [P, TT, 6]), sb("mv1", [P, TT, 2]), sb("rs1", [P, TT])
        st2, mv2, rs2 = sb("st2", [P, TT, 6]), sb("mv2", [P, TT, 2]), sb("rs2", [P, TT])
        st3, mv3, rs3 = sb("st3", [P, TT, 6]), sb("mv3", [P, TT, 2]), sb("rs3", [P, TT])
        z1 = sb("z1", [P, TT, D])
        xn = sb("xn", [P, KC, TOKENS])
        xn_s = sb("xn_s", [P, 2, KC, TOKENS], BF16)
        g = sb("g", [P, KC, TOKENS])
        gg = sb("gg", [P, KC, TOKENS])
        g_s = sb("g_s", [P, 2, KC, TOKENS], BF16)
        gg_s = sb("gg_s", [P, 2, KC, TOKENS], BF16)
        az = sb("az", [P, TOKENS])
        rz = sb("rz", [P, TOKENS])
        delta = sb("delta", [P, TOKENS])
        decay = sb("decay", [P, TOKENS])
        u = sb("u", [P, KC, TOKENS])
        q = sb("q", [P, KC, TOKENS])
        y = sb("y", [P, KC, TOKENS])
        y_s = sb("y_s", [P, 2, KC, TOKENS], BF16)
        x1 = sb("x1", [P, TT, D])
        z2 = sb("z2", [P, TT, D])
        xn2 = sb("xn2", [P, KC, TOKENS])
        xn2_s = sb("xn2_s", [P, 2, KC, TOKENS], BF16)
        HR = 4
        hf = sb("hf", [P, HR, TOKENS])
        h_s = sb("h_s", [P, 2, HC, TOKENS], BF16)
        v = sb("v", [P, TT, D])
        xp = sb("xp", [P, TT, D])

        bank = [pb(f"bank{k}", [P, 512]) for k in range(8)]

        def token_pair(k):
            return bank[k][:, :].rearrange("p (t d) -> p t d", t=2)

        vec_in, w_head, w_tail = sem("vec_in"), sem("w_head"), sem("w_tail")
        w_in = [sem("w_in_even"), sem("w_in_odd")]
        mean_done, ident_done = sem("mean_done"), sem("ident_done")
        x_loaded, x_used = sem("x_loaded"), sem("x_used")
        st1_r, mv1_r, ve1_r, rs1_r, z1_r = [sem(n) for n in ("st1_r", "mv1_r", "ve1_r", "rs1_r", "z1_r")]
        st2_r, mv2_r, ve2_r, rs2_r, z2_r = [sem(n) for n in ("st2_r", "mv2_r", "ve2_r", "rs2_r", "z2_r")]
        st3_r, mv3_r, ve3_r, rs3_r, xp_r = [sem(n) for n in ("st3_r", "mv3_r", "ve3_r", "rs3_r", "xp_r")]
        zT_done, xn_r, xn_head, xn_tail = [sem(n) for n in ("zT_done", "xn_r", "xn_head", "xn_tail")]
        gate_done, g_r, xg_r, g_head, g_tail, gg_head, gg_tail = [sem(n) for n in (
            "gate_done", "g_r", "xg_r", "g_head", "g_tail", "gg_head", "gg_tail")]
        zz_done, az_r, rz_r, ez_r, lz_r, delta_r, decay_r = [sem(n) for n in (
            "zz_done", "az_r", "rz_r", "ez_r", "lz_r", "delta_r", "decay_r")]
        u_done, b_done, u_r, q_r, dq_r, y_r, y_head, y_tail = [sem(n) for n in (
            "u_done", "b_done", "u_r", "q_r", "dq_r", "y_r", "y_head", "y_tail")]
        out_done, xob_r, xb2_r, x1_r, xres_r = [sem(n) for n in ("out_done", "xob_r", "xb2_r", "x1_r", "xres_r")]
        z2T_done, xn2_r, xn2_head, xn2_tail = [sem(n) for n in ("z2T_done", "xn2_r", "xn2_head", "xn2_tail")]
        m_done, hf_r, h_head, h_tail, o_done, v_r = [sem(n) for n in (
            "m_done", "hf_r", "h_head", "h_tail", "o_done", "v_r")]
        xp_stored, st_seen = sem("xp_stored"), sem("st_seen")

        LAST = BATCHES - 1
        LOOP0, LOOP1 = 2, 6

        def over_batches(eng, first, step, last):
            first()
            step(0, 0)
            step(1, 1)
            with eng.Fori(LOOP0, LOOP1, 2) as i:
                step(i, 0)
                step(i + 1, 1)
            step(LAST - 1, (LAST - 1) % 2)
            step(LAST, LAST % 2)
            last()

        def is_first(i):
            return isinstance(i, int) and i == 0

        def is_last(i):
            return isinstance(i, int) and i == LAST

        block = ctx.enter_context(nc.Block())

        @block.sync
        def _(sp):
            for tile, name in vectors:
                sp.dma_start(tile[:, :], t[name]).then_inc(vec_in, 16)

            def load_x(i, par):
                wait(sp, x_used, i - 1)
                wait(sp, x_loaded, 16 * i)
                sp.dma_start(x_in[:, par], t["x"][bass.ds(i, 1)].rearrange("b (t p) d -> p (b t) d", p=P))\
                    .then_inc(x_loaded, 16)

            load_x(0, 0)
            for n, (_, name, k, width) in enumerate(weights):
                wait(sp, w_tail, n - 1)
                sp.dma_start(staged[:, n % 2, 0:k * width].rearrange("p (k n) -> p k n", k=k),
                             t[name].rearrange("(k p) n -> p k n", p=P)).then_inc(w_in[n % 2], 16)

            def step(i, par):
                if not is_last(i):
                    load_x(i + 1, 1 - par)
                if not is_first(i):
                    store_xp(i - 1)

            def store_xp(j):
                sp.wait_ge(xp_r, 4 * j + 4)
                sp.dma_start(xp_dram[bass.ds(j, 1)].rearrange("b (t p) d -> p (b t) d", p=P), xp[:, :, :]).then_inc(xp_stored, 16)

            over_batches(sp, lambda: None, step, lambda: store_xp(LAST))
            sp.wait_ge(xp_stored, 16 * BATCHES)

        @block.gpsimd
        def _(pool):
            nc.gpsimd.memset(ident[:, :], 0.0).then_inc(ident_done, 1)
            nc.gpsimd.memset(neg_half[:, :], -0.5)
            nc.gpsimd.memset(eps_t[:, :], EPS).then_inc(ident_done, 1)
            pool.wait_ge(ident_done, 2)
            nc.gpsimd.affine_select(out=ident[:, :], in_=ident[:, :], compare_op=ALU.not_equal, fill=1.0,
                                    base=0, pattern=[[-1, P]], channel_multiplier=1).then_inc(ident_done, 1)
            pool.wait_ge(vec_in, 16 * len(vectors))

            def rstd(mv, ve_r, rs, rs_r, mv_r, b):
                pool.wait_ge(mv_r, TT * b + TT)
                nc.gpsimd.tensor_tensor(rs[:, :], mv[:, :, 1], eps_t[:, :], ALU.add).then_inc(ve_r, 1)
                pool.wait_ge(ve_r, b + 1)
                nc.gpsimd.tensor_tensor(rs[:, :], rs[:, :], neg_half[:, :], ALU.pow).then_inc(rs_r, 1)

            def bias_rows(i, par):
                pool.wait_ge(x_loaded, 16 * i + 16)
                wait(pool, x1_r, 2 * i)
                nc.gpsimd.tensor_tensor(x_ob[:, :, :], x_in[:, par], row4(out_b_row), ALU.add).then_inc(xob_r, 1)
                nc.gpsimd.tensor_tensor(x_b2[:, :, :], x_in[:, par], row4(mlp_b2_row), ALU.add).then_inc(xb2_r, 1)
                pool.wait_ge(xb2_r, i + 1)
                pool.wait_ge(xob_r, i + 1)
                pool.wait_ge(z1_r, TT * i + TT)
                pool.sem_inc(x_used, 1)

            def row4(row):
                return row[:, :].rearrange("p (a d) -> p a d", a=1).to_broadcast([P, TT, D])

            def residual(j):
                pool.wait_ge(x1_r, 2 * j + 2)
                pool.wait_ge(xb2_r, j + 1)
                wait(pool, v_r, 2 * j)
                nc.gpsimd.tensor_tensor(x_res[:, :, :], x1[:, :, :], x_b2[:, :, :], ALU.add).then_inc(xres_r, 1)
                pool.wait_ge(xres_r, j + 1)

            def step(i, par):
                if not is_first(i):
                    rstd(mv2, ve2_r, rs2, rs2_r, mv2_r, i - 1)
                    residual(i - 1)
                bias_rows(i, par)
                if not is_last(i):
                    rstd(mv1, ve1_r, rs1, rs1_r, mv1_r, i + 1)
                if not is_first(i):
                    rstd(mv3, ve3_r, rs3, rs3_r, mv3_r, i - 1)

            def last():
                rstd(mv2, ve2_r, rs2, rs2_r, mv2_r, LAST)
                residual(LAST)
                rstd(mv3, ve3_r, rs3, rs3_r, mv3_r, LAST)

            over_batches(pool, lambda: rstd(mv1, ve1_r, rs1, rs1_r, mv1_r, 0), step, last)

        @block.scalar
        def _(act):
            for n, (tile, _, k, width) in enumerate(weights):
                act.wait_ge(w_in[n % 2], 16 * (n // 2) + 16)
                nc.scalar.activation(tile[:, 0], staged[:, n % 2, 0:k * width].rearrange("p (k n) -> p k n", k=k),
                                     ACT.Copy).then_inc(w_head, 1)
            act.wait_ge(vec_in, 16 * len(vectors))
            act.wait_ge(mean_done, 5)

            def norm1(i):
                for c in range(KC):
                    act.wait_ge(zT_done, 2 * i + c + 1)
                    wait(act, xg_r, i)
                    wait(act, xn_tail, i)
                    nc.scalar.activation(xn[:, c], bank[c][:, :], ACT.Identity, bias=n1b[:, c:c + 1],
                                         scale=n1w[:, c:c + 1]).then_inc(xn_r, 1)

            def silus(i):
                for c in range(2 * KC):
                    act.wait_ge(gate_done, 4 * i + c + 1)
                    wait(act, g_tail if c < KC else gg_tail, i)
                    dst = g if c < KC else gg
                    nc.scalar.activation(dst[:, c % KC], bank[(2 + c) % 4][:, :], ACT.Silu,
                                         bias=gate_b[:, c:c + 1]).then_inc(g_r, 1)
                act.wait_ge(g_r, 4 * i + 4)
                wait(act, b_done, 2 * i)
                nc.scalar.activation(gg_s[:, 0], gg[:, :, :], ACT.Copy).then_inc(gg_head, 1)

            def norm2(j):
                for c in range(KC):
                    act.wait_ge(z2T_done, 2 * j + c + 1)
                    wait(act, xn2_tail, j)
                    nc.scalar.activation(xn2[:, c], bank[5 + c][:, :], ACT.Identity, bias=n2b[:, c:c + 1],
                                         scale=n2w[:, c:c + 1]).then_inc(xn2_r, 1)

            def decays(i):
                act.wait_ge(zz_done, i + 1)
                wait(act, delta_r, i)
                nc.scalar.activation(az[:, :], bank[4][:, :], ACT.Abs, bias=mean_b[:, :]).then_inc(az_r, 1)
                nc.scalar.activation(rz[:, :], bank[4][:, :], ACT.Relu, bias=mean_b[:, :]).then_inc(rz_r, 1)
                act.wait_ge(az_r, i + 1)
                nc.scalar.activation(az[:, :], az[:, :], ACT.Exp, scale=-1.0).then_inc(ez_r, 1)
                act.wait_ge(ez_r, i + 1)
                nc.scalar.activation(az[:, :], az[:, :], ACT.Ln, bias=1.0).then_inc(lz_r, 1)
                act.wait_ge(delta_r, i + 1)
                wait(act, y_r, 2 * i)
                nc.scalar.activation(decay[:, :], delta[:, :], ACT.Exp, scale=-1.0).then_inc(decay_r, 1)

            def gelus(j):
                for k in range(HC):
                    act.wait_ge(m_done, HC * j + k + 1)
                    wait(act, h_tail, HC * j + k + 1 - HR)
                    nc.scalar.activation(hf[:, k % HR], bank[5 + (2 + k) % 3][:, :], ACT.Gelu,
                                         bias=mlp_b1[:, k:k + 1]).then_inc(hf_r, 1)
                    act.wait_ge(hf_r, HC * j + k + 1)
                    nc.scalar.activation(h_s[:, 0, k], hf[:, k % HR], ACT.Copy).then_inc(h_head, 1)

            def us(i):
                for c in range(KC):
                    act.wait_ge(u_done, 2 * i + c + 1)
                    wait(act, q_r, 2 * i)
                    nc.scalar.activation(u[:, c], bank[2 + c][:, :], ACT.Identity,
                                         bias=state_b[:, c:c + 1]).then_inc(u_r, 1)

            def y_heads(i):
                act.wait_ge(y_r, 2 * i + 2)
                wait(act, out_done, 2 * i)
                nc.scalar.activation(y_s[:, 0], y[:, :, :], ACT.Copy).then_inc(y_head, 1)

            def step(i, par):
                silus(i)
                if not is_first(i):
                    norm2(i - 1)
                decays(i)
                if not is_first(i):
                    gelus(i - 1)
                us(i)
                y_heads(i)
                if not is_last(i):
                    norm1(i + 1)

            def last():
                norm2(LAST)
                gelus(LAST)

            over_batches(act, lambda: norm1(0), step, last)

        @block.vector
        def _(dve):
            dve.wait_ge(vec_in, 16 * len(vectors))
            nc.vector.reduce_sum(mean_b[:, :], state_b_row[:, :], AX.X).then_inc(mean_done, 1)
            dve.wait_ge(mean_done, 1)
            nc.vector.tensor_scalar(mean_b[:, :], mean_b[:, :], 1.0 / D, None, ALU.mult).then_inc(mean_done, 1)
            for n, (tile, name, k, width) in enumerate(weights):
                src = staged[:, n % 2, 0:k * width].rearrange("p (k n) -> p k n", k=k)
                if name == "state_w":
                    dve.wait_ge(w_in[n % 2], 16 * (n // 2) + 16)
                    nc.vector.reduce_sum(mean_col[:, :], src, AX.X).then_inc(mean_done, 1)
                dve.wait_ge(w_head, n + 1)
                nc.vector.tensor_tensor(tile[:, 1], src, tile[:, 0], ALU.subtract).then_inc(w_tail, 1)
            dve.wait_ge(mean_done, 3)
            nc.vector.tensor_scalar(mean_full[:, :, :],
                                    mean_col[:, :].rearrange("p (k a) -> p k a", a=1).to_broadcast([P, KC, P]),
                                    1.0 / D, None, ALU.mult).then_inc(mean_done, 1)
            dve.wait_ge(mean_done, 4)
            nc.vector.tensor_copy(mean_w[:, 0], mean_full[:, :, :]).then_inc(mean_done, 1)
            dve.wait_ge(mean_done, 5)
            nc.vector.tensor_tensor(mean_w[:, 1], mean_full[:, :, :], mean_w[:, 0], ALU.subtract)\
                .then_inc(mean_done, 1)

            def stats(src, st, st_r, mv, mv_r, b, free):
                for n in range(TT):
                    nc.vector.bn_stats(st[:, n], src[:, n]).then_inc(st_r, 1)
                dve.wait_ge(st_r, TT * b + TT)
                dve.sem_inc(st_seen, 1)
                for n in range(TT):
                    nc.vector.bn_aggr(mv[:, n], st[:, n]).then_inc(mv_r, 1)

            def normalise(dst, src, mv, rs, rs_r, done, b):
                dve.wait_ge(rs_r, b + 1)
                for n in range(TT):
                    nc.vector.tensor_scalar(dst[:, n], src[:, n], mv[:, n, 0:1], rs[:, n:n + 1],
                                            ALU.subtract, ALU.mult).then_inc(done, 1)

            def split(dst, src, head, tail, b):
                nc.vector.tensor_copy(dst[:, 0], src).then_inc(head, 1)
                dve.wait_ge(head, b + 1)
                nc.vector.tensor_tensor(dst[:, 1], src, dst[:, 0], ALU.subtract).then_inc(tail, 1)

            def norm1(i, par):
                dve.wait_ge(x_loaded, 16 * i + 16)
                wait(dve, rs1_r, i)
                stats(x_in[:, par], st1, st1_r, mv1, mv1_r, i, None)
                wait(dve, zT_done, 2 * i)
                normalise(z1, x_in[:, par], mv1, rs1, rs1_r, z1_r, i)

            def norm1_split(i):
                dve.wait_ge(xn_r, 2 * i + 2)
                wait(dve, zz_done, i)
                split(xn_s, xn[:, :, :], xn_head, xn_tail, i)

            def norm2(j):
                for h in range(2):
                    dve.wait_ge(out_done, 2 * j + h + 1)
                    dve.wait_ge(xob_r, j + 1)
                    wait(dve, xres_r, j)
                    nc.vector.tensor_tensor(x1[:, 2 * h:2 * h + 2], token_pair(2 + h), x_ob[:, 2 * h:2 * h + 2],
                                            ALU.add).then_inc(x1_r, 1)
                dve.wait_ge(x1_r, 2 * j + 2)
                stats(x1, st2, st2_r, mv2, mv2_r, j, None)
                wait(dve, z2T_done, 2 * j)
                normalise(z2, x1, mv2, rs2, rs2_r, z2_r, j)

            def norm2_split(j):
                dve.wait_ge(xn2_r, 2 * j + 2)
                wait(dve, m_done, HC * j)
                split(xn2_s, xn2[:, :, :], xn2_head, xn2_tail, j)

            def gates(i):
                dve.wait_ge(g_r, 4 * i + 2)
                nc.vector.tensor_tensor(g[:, :, :], g[:, :, :], xn[:, :, :], ALU.mult).then_inc(xg_r, 1)
                dve.wait_ge(xg_r, i + 1)
                wait(dve, u_done, 2 * i)
                split(g_s, g[:, :, :], g_head, g_tail, i)
                dve.wait_ge(gg_head, i + 1)
                nc.vector.tensor_tensor(gg_s[:, 1], gg[:, :, :], gg_s[:, 0], ALU.subtract).then_inc(gg_tail, 1)
                dve.wait_ge(lz_r, i + 1)
                dve.wait_ge(rz_r, i + 1)
                wait(dve, dq_r, 2 * i)
                wait(dve, decay_r, i)
                nc.vector.tensor_tensor(delta[:, :], rz[:, :], az[:, :], ALU.add).then_inc(delta_r, 1)

            def gelu_tails(j):
                for k in range(HC):
                    dve.wait_ge(h_head, HC * j + k + 1)
                    nc.vector.tensor_tensor(h_s[:, 1, k], hf[:, k % HR], h_s[:, 0, k], ALU.subtract)\
                        .then_inc(h_tail, 1)

            def scans(i):
                for c in range(KC):
                    dve.wait_ge(b_done, 2 * i + c + 1)
                    dve.wait_ge(u_r, 2 * i + c + 1)
                    nc.vector.scalar_tensor_tensor(q[:, c], bank[c][:, :], state_b[:, c:c + 1], u[:, c],
                                                   ALU.add, ALU.mult).then_inc(q_r, 1)
                for c in range(KC):
                    dve.wait_ge(q_r, 2 * i + c + 1)
                    nc.vector.tensor_tensor(q[:, c], q[:, c], delta[:, :], ALU.mult).then_inc(dq_r, 1)
                for c in range(KC):
                    dve.wait_ge(dq_r, 2 * i + c + 1)
                    dve.wait_ge(decay_r, i + 1)
                    wait(dve, y_tail, i)
                    nc.vector.tensor_tensor_scan(y[:, c], decay[:, :], q[:, c], 0.0, ALU.mult, ALU.add)\
                        .then_inc(y_r, 1)
                dve.wait_ge(y_head, i + 1)
                nc.vector.tensor_tensor(y_s[:, 1], y[:, :, :], y_s[:, 0], ALU.subtract).then_inc(y_tail, 1)

            def norm3(j):
                dve.wait_ge(xres_r, j + 1)
                for h in range(2):
                    dve.wait_ge(o_done, 2 * j + h + 1)
                    wait(dve, xp_r, 4 * j)
                    nc.vector.tensor_tensor(v[:, 2 * h:2 * h + 2], token_pair(6 + h), x_res[:, 2 * h:2 * h + 2],
                                            ALU.add).then_inc(v_r, 1)
                dve.wait_ge(v_r, 2 * j + 2)
                stats(v, st3, st3_r, mv3, mv3_r, j, None)
                wait(dve, xp_stored, 16 * j)
                normalise(xp, v, mv3, rs3, rs3_r, xp_r, j)

            def first():
                norm1(0, 0)
                norm1_split(0)

            def step(i, par):
                if not is_first(i):
                    norm2(i - 1)
                gates(i)
                if not is_first(i):
                    norm2_split(i - 1)
                    gelu_tails(i - 1)
                if not is_last(i):
                    norm1(i + 1, 1 - par)
                scans(i)
                if not is_last(i):
                    norm1_split(i + 1)
                if not is_first(i):
                    norm3(i - 1)

            def last():
                norm2(LAST)
                norm2_split(LAST)
                gelu_tails(LAST)
                norm3(LAST)

            over_batches(dve, first, step, last)

        @block.tensor
        def _(pe):
            pe.wait_ge(ident_done, 3)

            def turn(src, banks, done):
                for c in range(KC):
                    for n in range(TT):
                        last = nc.tensor.transpose(bank[banks[c]][:, n * P:(n + 1) * P],
                                                   src[:, n, c * P:(c + 1) * P], ident[:, :])
                    last.then_inc(done, 1)

            def turn1(i):
                pe.wait_ge(z1_r, TT * i + TT)
                wait(pe, q_r, 2 * i)
                turn(z1, (0, 1), zT_done)

            def gates(i):
                pe.wait_ge(xn_tail, i + 1)
                for c in range(2 * KC):
                    wait(pe, x1_r, 2 * i)
                    split_product(nc, bank[(2 + c) % 4][:, :], lambda s, k: gate_w[:, s, k, c * P:(c + 1) * P],
                                  lambda s, k: xn_s[:, s, k], KC).then_inc(gate_done, 1)
                wait(pe, az_r, i)
                wait(pe, rz_r, i)
                split_product(nc, bank[4][:, :], lambda s, k: mean_w[:, s, k], lambda s, k: xn_s[:, s, k], KC)\
                    .then_inc(zz_done, 1)

            def turn2(j):
                pe.wait_ge(z2_r, TT * j + TT)
                wait(pe, hf_r, HC * j)
                wait(pe, v_r, 2 * j)
                turn(z2, (5, 6), z2T_done)

            def mlp_up(j):
                pe.wait_ge(xn2_tail, j + 1)
                for m in range(HC):
                    if m >= 3:
                        pe.wait_ge(hf_r, HC * j + m - 2)
                    split_product(nc, bank[5 + (2 + m) % 3][:, :], lambda s, k: mlp_w1[:, s, k, m * P:(m + 1) * P],
                                  lambda s, k: xn2_s[:, s, k], KC).then_inc(m_done, 1)

            def states(i):
                pe.wait_ge(g_tail, i + 1)
                pe.wait_ge(g_r, 4 * i + 4)
                for c in range(KC):
                    split_product(nc, bank[2 + c][:, :], lambda s, k: state_w[:, s, k, c * P:(c + 1) * P],
                                  lambda s, k: g_s[:, s, k], KC).then_inc(u_done, 1)
                pe.wait_ge(gg_tail, i + 1)
                for c in range(KC):
                    split_product(nc, bank[c][:, :], lambda s, k: state_w[:, s, k, c * P:(c + 1) * P],
                                  lambda s, k: gg_s[:, s, k], KC).then_inc(b_done, 1)

            def mlp_down(j):
                pe.wait_ge(h_tail, HC * j + HC)
                for h in range(2):
                    for n in (2 * h, 2 * h + 1):
                        last = split_product(nc, token_pair(6 + h)[:, n % 2], lambda s, k: h_s[:, s, k, n * P:(n + 1) * P],
                                             lambda s, k: mlp_w2[:, s, k], HC)
                    last.then_inc(o_done, 1)

            def project(i):
                pe.wait_ge(y_tail, i + 1)
                for h in range(2):
                    pe.wait_ge(u_r, 2 * i + h + 1)
                    for n in (2 * h, 2 * h + 1):
                        last = split_product(nc, token_pair(2 + h)[:, n % 2], lambda s, k: y_s[:, s, k, n * P:(n + 1) * P],
                                             lambda s, k: out_w[:, s, k], KC)
                    last.then_inc(out_done, 1)

            def step(i, par):
                if is_first(i):
                    pe.wait_ge(w_tail, len(weights))
                    pe.wait_ge(mean_done, 6)
                gates(i)
                if not is_first(i):
                    turn2(i - 1)
                    mlp_up(i - 1)
                states(i)
                if not is_first(i):
                    mlp_down(i - 1)
                if not is_last(i):
                    turn1(i + 1)
                project(i)

            def last():
                turn2(LAST)
                mlp_up(LAST)
                mlp_down(LAST)

            over_batches(pe, lambda: turn1(0), step, last)


NE, FE = 8, 512
FC = FE // P
NTILES = BATCHES * TT
SLOT = 256
ST = SLOT // P
QT = (2 * NTILES * P // SLOT + NE - 1 + 1) // 2 * 2
GENS = 3
SQ_MAX = 20

R177 = 177.0 ** 0.5
C3 = 2.0 / 3.0
C1, C2 = C3 * (1 + R177) / 88, C3 * (1 + R177) / 352
C4 = (-271 + 29 * R177) / (315 * C3)
C5, C6 = 11 * (-1 + R177) / (1260 * C3), 11 * (-9 + R177) / (5040 * C3)
C7 = (89 - R177) / (5040 * C3 * C3)
CY2 = (857 - 58 * R177) / 630


def moe_half(nc, t, xp_dram, ab_dram, zs_dram, ys_dram, out):
    keep = ExitStack()
    with keep:
        def ksb(name, shape, dt=F32):
            return keep.enter_context(nc.sbuf_tensor(name, shape, dt))

        ident = ksb("ident_b", [P, P])
        w1_s = ksb("w1_s", [P, 2, NE * KC * FE], BF16)
        w2_s = ksb("w2_s", [P, 2, NE * FC * D], BF16)
        eb1 = ksb("eb1", [P, NE * FC])
        eb2r = ksb("eb2r", [NE, D])
        eb2 = ksb("eb2", [NE, D])
        gamma, beta = ksb("gamma", [P, KC]), ksb("beta", [P, KC])
        gc1_row, gc2_row, gc_b = ksb("gc1_row", [P, D]), ksb("gc2_row", [P, D]), ksb("gc_b", [P, 1])
        neg_half = ksb("neg_half_b", [P, TT])
        eps_t = ksb("eps_t_b", [P, TT])
        wdense = ksb("wdense", [P, NTILES, NE])
        wtop = ksb("wtop", [P, 2, NTILES])
        pos = ksb("pos", [P, 2, NTILES], U32)
        tile_expert = ksb("tile_expert", [P, QT], I32)
        plan(nc, t, locals(), xp_dram, ab_dram, zs_dram)
        experts(nc, locals(), zs_dram, ys_dram)
        combine(nc, locals(), xp_dram, ab_dram, ys_dram, out)


def plan(nc, t, kept, xp_dram, ab_dram, zs_dram):
    (ident, w1_s, w2_s, eb1, eb2r, eb2, gamma, beta, gc1_row, gc2_row, gc_b, neg_half, eps_t, wdense, wtop, pos,
     tile_expert) = [kept[n] for n in (
        "ident", "w1_s", "w2_s", "eb1", "eb2r", "eb2", "gamma", "beta", "gc1_row", "gc2_row", "gc_b",
        "neg_half", "eps_t", "wdense", "wtop", "pos", "tile_expert")]
    ctx = ExitStack()
    with ctx:
        def sb(name, shape, dt=F32):
            return ctx.enter_context(nc.sbuf_tensor(name, shape, dt))

        def pb(name, shape, dt=F32):
            return ctx.enter_context(nc.psum_tensor(name, shape, dt))

        def sem(name):
            return ctx.enter_context(nc.semaphore(name))

        bank = [pb(f"pbank{k}", [P, 512]) for k in range(8)]
        tri, ones = sb("tri", [P, P], BF16), sb("ones", [P, P], BF16)
        ones32 = sb("ones32", [P, NTILES])
        zero = sb("zero", [P, 1024])
        iota8i, iota8 = sb("iota8i", [P, NE], I32), sb("iota8", [P, NE])
        iota16i, iota16 = sb("iota16i", [P, 16], I32), sb("iota16", [P, 16])
        iotaqi, iotaq = sb("iotaqi", [P, QT], I32), sb("iotaq", [P, QT])
        thr = sb("thr", [P, SQ_MAX - 1])
        A, A2, U, L, X = [sb(n, [P, GENS, KC, D]) for n in ("gA", "gA2", "gU", "gL", "gX")]
        aT_s, b_s = [sb(n, [P, GENS, 2, KC, D], BF16) for n in ("aT_s", "b_s")]
        rows_sum, norm, hits = sb("rows_sum", [P, GENS * KC]), sb("norm", [P, 2]), sb("hits", [P, SQ_MAX - 1])
        sq_f, sq_i = sb("sq_f", [P, 3]), sb("sq_i", [P, 2], I32)
        w1_f = sb("w1_f", [P, 2, KC * FE])
        w2t_f = sb("w2t_f", [P, 2, KC * FE])
        w2_f = sb("w2_f", [P, 2, FC * D])
        w2t_s = sb("w2t_s", [P, 2, 2, KC * FE], BF16)
        eb2t = sb("eb2t", [P, KC, NE])
        abel_f, abel_s, abel_b = sb("abel_f", [P, KC, D]), sb("abel_s", [P, 2, KC, D], BF16), sb("abel_b", [P, D])
        mgw, mgb = sb("mgw", [P, KC, NE]), sb("mgb", [P, NE])
        xp = sb("xp_b", [P, 2, TT, D])
        st, mv, rs = sb("st_b", [P, TT, 6]), sb("mv_b", [P, TT, 2]), sb("rs_b", [P, TT])
        z3 = sb("z3", [P, NTILES, D])
        xn3 = A2[:, 0:2].rearrange("p g c d -> p g (c d)")
        xn3_s = U[:, 0:2].bitcast(BF16)
        abel = A[:, 0:2].rearrange("p g c d -> p (g c) d")
        logits = sb("logits", [P, NTILES, NE])
        top = sb("top", [P, NTILES, 8])
        topi = sb("topi", [P, NTILES, 8], U32)
        topf = sb("topf", [P, 2, NTILES])
        oh = sb("oh", [P, 2, NTILES, NE])
        picked = sb("picked", [P, NTILES, NE], BF16)
        tot, cum, slot, prod = [sb(n, [P, NTILES, NE]) for n in ("tot", "cum", "slot", "prod")]
        ntile, cumt, base = sb("ntile", [P, NE]), sb("cumt", [P, NE]), sb("base", [P, NE])
        over, below = sb("over", [P, NE, 16]), sb("below", [P, QT, NE])
        tef, posf = sb("tef", [P, QT]), sb("posf", [P, NTILES])
        td = sb("td", [P, NTILES])

        vec_in, gens_in, const_done, zs_zero = [sem(n) for n in ("p_vec_in", "p_gens_in", "p_const", "p_zs_zero")]
        norm_r, all_norm, sq_r, step = [sem(n) for n in ("p_norm_r", "p_all_norm", "p_sq_r", "p_step")]
        mat_r, b_head, turned, a_head, split_r, prod_done = [sem(n) for n in (
            "p_mat_r", "p_b_head", "p_turned", "p_a_head", "p_split_r", "p_prod_done")]
        w_in = [sem("p_w_in0"), sem("p_w_in1")]
        w_head, w_tail, fold_done, w2_r, w2_head, w2_tail = [sem(n) for n in (
            "p_w_head", "p_w_tail", "p_fold_done", "p_w2_r", "p_w2_head", "p_w2_tail")]
        eb_done, eb_r, st_seen = sem("p_eb_done"), sem("p_eb_r"), sem("p_st_seen")
        xp_in, st_r, mv_r, ve_r, rs_r, z3_r = [sem(n) for n in (
            "p_xp_in", "p_st_r", "p_mv_r", "p_ve_r", "p_rs_r", "p_z3_r")]
        zT_done, xn_r, xn_head, xn_tail, lg_done, lg_r, ab_done, ab_r, gelu_r, ab_stored, top_r = [sem(n) for n in (
            "p_zT_done", "p_xn_r", "p_xn_head", "p_xn_tail", "p_lg_done", "p_lg_r", "p_ab_done", "p_ab_r",
            "p_gelu_r", "p_ab_stored", "p_top_r")]
        gap_r, gap_exp, picked_r, rank_done, pos_r, sent = [sem(n) for n in (
            "p_gap_r", "p_gap_exp", "p_picked_r", "p_rank_done", "p_pos_r", "p_sent")]

        vectors = [(ident, "ident"), (eb1, "eb1"), (eb2, "eb2"), (gamma, "gamma"), (beta, "beta"),
                   (gc1_row, "gc1_row"), (gc2_row, "gc2_row"), (gc_b, "gc_b"), (abel_b, "abel_b"), (mgb, "mgb")]
        vectors = [(a, n) for a, n in vectors if n != "ident"]
        NV = 16 * (len(vectors) + 3)

        def pair(k):
            return bank[k][:, :].rearrange("p (t d) -> p t d", t=2)

        def mat(k):
            return bank[k][:, :].rearrange("p (c d) -> p c d", c=KC)

        def of_tile(x, b):
            return x[:, bass.ds(b * TT, TT)]

        block = ctx.enter_context(nc.Block())

        @block.sync
        def _(sp):
            for tile, name in vectors:
                sp.dma_start(tile[:, :], t[name]).then_inc(vec_in, 16)
            sp.dma_start(eb2t[:, :, :], t["eb2t"].rearrange("(k p) n -> p k n", p=P)).then_inc(vec_in, 16)
            sp.dma_start(mgw[:, :, :], t["mgw"].rearrange("(k p) n -> p k n", p=P)).then_inc(vec_in, 16)
            sp.dma_start(abel_f[:, :, :], t["abel_w"].rearrange("(k p) n -> p k n", p=P)).then_inc(vec_in, 16)
            sp.dma_start(A[:, :, :, :], t["gens"].rearrange("g (k p) n -> p g k n", p=P)).then_inc(gens_in, 16)

            def load_expert(e, par):
                wait(sp, w2_tail, e - 1)
                sp.dma_start(w1_f[:, par].rearrange("p (k n) -> p k n", k=KC),
                             t["ew1"][bass.ds(e, 1)].rearrange("e (k p) n -> p (e k) n", p=P)).then_inc(w_in[par], 16)
                sp.dma_start(w2t_f[:, par].rearrange("p (k n) -> p k n", k=KC),
                             t["ew2t"][bass.ds(e, 1)].rearrange("e (k p) n -> p (e k) n", p=P)).then_inc(w_in[par], 16)
                sp.dma_start(w2_f[:, par].rearrange("p (k n) -> p k n", k=FC),
                             t["ew2"][bass.ds(e, 1)].rearrange("e (k p) n -> p (e k) n", p=P)).then_inc(w_in[par], 16)

            load_expert(0, 0)
            load_expert(1, 1)
            sp.wait_ge(const_done, 1)
            rows = QT * SLOT * D // (P * 1024)
            zv = zs_dram.rearrange("(a p c) d -> a p (c d)", p=P, a=rows)
            for a in range(rows):
                sp.dma_start(zv[a], zero[:, :]).then_inc(zs_zero, 16)
            with sp.Fori(2, NE - 1, 2) as e:
                load_expert(e, 0)
                load_expert(e + 1, 1)

            def load_xp(b, par):
                wait(sp, z3_r, TT * (b - 1))
                wait(sp, xp_in, 16 * b)
                sp.dma_start(xp[:, par], xp_dram[bass.ds(b, 1)].rearrange("b (t p) d -> p (b t) d", p=P))\
                    .then_inc(xp_in, 16)

            def store_abel(b):
                sp.wait_ge(gelu_r, TT // 2 * (b + 1))
                sp.dma_start(ab_dram[bass.ds(b, 1)].rearrange("b (t p) d -> p (b t) d", p=P), abel[:, :, :])\
                    .then_inc(ab_stored, 16)

            load_xp(0, 0)
            load_xp(1, 1)
            store_abel(0)
            load_xp(2, 0)
            store_abel(1)
            with sp.Fori(2, BATCHES - 3, 2) as b:
                load_xp(b + 1, 1)
                store_abel(b)
                load_xp(b + 2, 0)
                store_abel(b + 1)
            load_xp(BATCHES - 1, 1)
            store_abel(BATCHES - 2)
            store_abel(BATCHES - 1)
            sp.wait_ge(ab_stored, 16 * BATCHES)
            sp.wait_ge(zs_zero, 16 * rows)

        ROWS = QT * SLOT * D // (P * 1024)

        @block.gpsimd
        def _(pool):
            nc.gpsimd.memset(zero[:, :], 0.0).then_inc(const_done, 1)
            nc.gpsimd.memset(ident[:, :], 0.0)
            nc.gpsimd.memset(neg_half[:, :], -0.5)
            nc.gpsimd.memset(eps_t[:, :], EPS)
            nc.gpsimd.memset(tri[:, :], 1.0)
            nc.gpsimd.memset(ones[:, :], 1.0)
            nc.gpsimd.memset(ones32[:, :], 1.0)
            for k in range(SQ_MAX - 1):
                nc.gpsimd.memset(thr[:, k:k + 1], float(2 ** k))
            nc.gpsimd.iota(iota8i[:, :], [[1, NE]], base=0, channel_multiplier=0)
            nc.gpsimd.iota(iota16i[:, :], [[1, 16]], base=0, channel_multiplier=0)
            nc.gpsimd.iota(iotaqi[:, :], [[1, QT]], base=0, channel_multiplier=0).then_inc(const_done, 1)
            pool.wait_ge(const_done, 2)
            nc.gpsimd.affine_select(out=ident[:, :], in_=ident[:, :], compare_op=ALU.not_equal, fill=1.0,
                                    base=0, pattern=[[-1, P]], channel_multiplier=1)
            nc.gpsimd.affine_select(out=tri[:, :], in_=tri[:, :], compare_op=ALU.is_gt, fill=0.0,
                                    base=0, pattern=[[1, P]], channel_multiplier=-1).then_inc(const_done, 1)
            pool.wait_ge(const_done, 3)
            pool.wait_ge(norm_r, 2)

            nc.gpsimd.partition_all_reduce(norm[:, 1:2], norm[:, 0:1], P, bass.bass_isa.ReduceOp.max)\
                .then_inc(all_norm, 1)

            def rstd(b):
                pool.wait_ge(mv_r, TT * b + TT)
                nc.gpsimd.tensor_tensor(rs[:, :], mv[:, :, 1], eps_t[:, :], ALU.add).then_inc(ve_r, 1)
                pool.wait_ge(ve_r, b + 1)
                nc.gpsimd.tensor_tensor(rs[:, :], rs[:, :], neg_half[:, :], ALU.pow).then_inc(rs_r, 1)

            with pool.Fori(0, BATCHES) as b:
                rstd(b)
            pool.wait_ge(zs_zero, 16 * ROWS)
            pool.wait_ge(pos_r, 2)
            for r in range(2):
                for n in range(NTILES):
                    nc.gpsimd.indirect_dma_start(
                        out=zs_dram[:, :], out_offset=bass.IndirectOffsetOnAxis(ap=pos[:, r, n:n + 1], axis=0),
                        in_=z3[:, n, :], in_offset=None).then_inc(sent, 16)
            pool.wait_ge(sent, 16 * 2 * NTILES)

        def expm_order(eng, one, count):
            for n in range(3 * GENS):
                one(n, n % GENS, None)
            return count

        @block.scalar
        def _(act):
            act.wait_ge(vec_in, NV)
            nc.scalar.activation(abel_s[:, 0], abel_f[:, :, :], ACT.Copy).then_inc(w_head, 1)

            def heads(n, slot, need, a_slot):
                act.wait_ge(mat_r, need)
                nc.scalar.activation(b_s[:, slot, 0], b_of(n, slot), ACT.Copy).then_inc(b_head, 1)
                act.wait_ge(turned, n + 1)
                nc.scalar.activation(aT_s[:, slot, 0], mat(slot), ACT.Copy).then_inc(a_head, 1)

            def b_of(n, slot):
                if isinstance(n, int):
                    return (A, U, U)[n // GENS][:, slot]
                return X[:, slot]

            for n in range(3 * GENS):
                heads(n, n % GENS, n + 1, None)
            act.wait_ge(sq_r, 4)
            squarings = act.value_load(sq_i[0:1, 0:1], min_val=1, max_val=SQ_MAX)
            with act.Fori(0, squarings) as k:
                for s in range(GENS):
                    heads(k * GENS + (3 * GENS + s), s, k * GENS + (3 * GENS + s + 1), None)
            after = squarings * GENS + 3 * GENS
            heads(after, 1, after + 3, 0)
            heads(after + 1, 2, after + 4, 1)
            act.wait_ge(mat_r, after + 5)
            nc.scalar.activation(b_s[:, 0, 0], L[:, 0], ACT.Copy).then_inc(b_head, 1)

            def expert_heads(e, par):
                act.wait_ge(w_in[par], (e - par) * 24 + 48)
                nc.scalar.activation(w1_s[:, 0, bass.ds(e * (KC * FE), KC * FE)], w1_f[:, par], ACT.Copy)\
                    .then_inc(w_head, 1)
                wait(act, fold_done, 2 * (e - 1))
                nc.scalar.activation(w2t_s[:, par, 0], w2t_f[:, par], ACT.Copy).then_inc(w_head, 1)

            def folded_heads(e, par):
                act.wait_ge(w2_r, 2 * e + 2)
                nc.scalar.activation(w2_s[:, 0, bass.ds(e * (FC * D), FC * D)], w2_f[:, par], ACT.Copy)\
                    .then_inc(w2_head, 1)

            for e in (0, 1):
                expert_heads(e, e)
                folded_heads(e, e)
            with act.Fori(2, NE - 1, 2) as e:
                for par in range(2):
                    expert_heads(e + par, par)
                    folded_heads(e + par, par)

            def norm(b):
                for c in range(KC):
                    act.wait_ge(zT_done, 2 * b + c + 1)
                    wait(act, xn_tail, b)
                    wait(act, lg_done, b)
                    nc.scalar.activation(xn3[:, c], bank[c][:, :], ACT.Identity, bias=beta[:, c:c + 1],
                                         scale=gamma[:, c:c + 1]).then_inc(xn_r, 1)

            def gelus(b):
                for h in range(2):
                    act.wait_ge(ab_r, 2 * b + h + 1)
                    nc.scalar.activation(abel[:, 2 * h:2 * h + 2], abel[:, 2 * h:2 * h + 2], ACT.Gelu)\
                        .then_inc(gelu_r, 1)

            norm(0)
            gelus(0)
            with act.Fori(1, BATCHES) as b:
                norm(b)
                gelus(b)
            act.wait_ge(gap_r, 1)
            nc.scalar.activation(td[:, :], td[:, :], ACT.Exp).then_inc(gap_exp, 1)

        @block.vector
        def _(dve):
            links = [0]

            def link(*ins):
                for i in ins:
                    i.then_inc(step, 1)
                links[0] += len(ins)
                dve.wait_ge(step, links[0])

            dve.wait_ge(vec_in, NV)
            dve.wait_ge(w_head, 1)
            nc.vector.tensor_tensor(abel_s[:, 1], abel_f[:, :, :], abel_s[:, 0], ALU.subtract).then_inc(w_tail, 1)
            dve.wait_ge(gens_in, 16)
            nc.vector.tensor_reduce(rows_sum[:, :], A[:, :, :, :].rearrange("p g k n -> p (g k) n"), AX.X, ALU.add,
                                    apply_absolute_value=True).then_inc(norm_r, 1)
            dve.wait_ge(norm_r, 1)
            nc.vector.reduce_max(norm[:, 0:1], rows_sum[:, :], AX.X).then_inc(norm_r, 1)
            dve.wait_ge(const_done, 3)
            dve.wait_ge(all_norm, 1)
            link(nc.vector.tensor_scalar(hits[:, :], thr[:, :], norm[:, 1:2], None, ALU.is_lt))
            nc.vector.reduce_sum(sq_f[:, 0:1], hits[:, :], AX.X).then_inc(sq_r, 1)
            dve.wait_ge(sq_r, 1)
            nc.vector.tensor_scalar(sq_f[:, 1:2], sq_f[:, 0:1], 1.0, None, ALU.add).then_inc(sq_r, 1)
            dve.wait_ge(sq_r, 2)
            nc.vector.tensor_scalar(sq_f[:, 2:3], sq_f[:, 1:2], -float(2 ** 23), float(127 * 2 ** 23),
                                    ALU.mult, ALU.add).then_inc(sq_r, 1)
            dve.wait_ge(sq_r, 3)
            nc.vector.tensor_copy(sq_i[:, :], sq_f[:, 1:3]).then_inc(sq_r, 1)
            dve.wait_ge(sq_r, 4)
            for s in range(GENS):
                nc.vector.tensor_scalar(A[:, s], A[:, s], sq_i[:, 1:2].bitcast(F32), None, ALU.mult)\
                    .then_inc(mat_r, 1)

            def tails(n, slot, src, need):
                dve.wait_ge(mat_r, need)
                dve.wait_ge(b_head, n + 1)
                nc.vector.tensor_tensor(b_s[:, slot, 1], src, b_s[:, slot, 0], ALU.subtract).then_inc(split_r, 1)
                dve.wait_ge(a_head, n + 1)
                nc.vector.tensor_tensor(aT_s[:, slot, 1], mat(slot), aT_s[:, slot, 0], ALU.subtract)\
                    .then_inc(split_r, 1)

            def stt(dst, x, c, z):
                return nc.vector.scalar_tensor_tensor(dst, x, c, z, ALU.mult, ALU.add)

            for s in range(GENS):
                tails(s, s, A[:, s], s + 1)
            for s in range(GENS):
                dve.wait_ge(prod_done, s + 1)
                link(nc.vector.tensor_copy(A2[:, s], mat(3 + s)),
                     nc.vector.tensor_scalar(U[:, s], A[:, s], C1, None, ALU.mult))
                stt(U[:, s], A2[:, s], C2, U[:, s]).then_inc(mat_r, 1)
            for s in range(GENS):
                tails(GENS + s, s, U[:, s], GENS + s + 1)
            for s in range(GENS):
                dve.wait_ge(prod_done, GENS + s + 1)
                link(stt(L[:, s], A2[:, s], C3, mat(3 + s)),
                     nc.vector.tensor_scalar(U[:, s], A[:, s], C5, None, ALU.mult))
                link(stt(U[:, s], A2[:, s], C6 - C7 * C3, U[:, s]))
                stt(U[:, s], L[:, s], C7, U[:, s]).then_inc(mat_r, 1)
            for s in range(GENS):
                tails(2 * GENS + s, s, U[:, s], 2 * GENS + s + 1)
                link(stt(X[:, s], A2[:, s], CY2, A[:, s]))
                link(stt(X[:, s], L[:, s], C4, X[:, s]))
            for s in range(GENS):
                dve.wait_ge(prod_done, 2 * GENS + s + 1)
                nc.vector.tensor_tensor(X[:, s], X[:, s], mat(3 + s), ALU.add).then_inc(mat_r, 1)
            squarings = dve.value_load(sq_i[0:1, 0:1], min_val=1, max_val=SQ_MAX)
            with dve.Fori(0, squarings) as k:
                for s in range(GENS):
                    tails(k * GENS + (3 * GENS + s), s, X[:, s], k * GENS + (3 * GENS + s + 1))
                for s in range(GENS):
                    dve.wait_ge(prod_done, k * GENS + (3 * GENS + s + 1))
                    stt(X[:, s], X[:, s], 2.0, mat(3 + s)).then_inc(mat_r, 1)
            after = squarings * GENS + 3 * GENS
            dve.wait_ge(mat_r, after + 3)
            link(nc.vector.tensor_tensor(L[:, 0], X[:, 0], X[:, 1], ALU.add))
            tails(after, 1, X[:, 1], after + 3)
            dve.wait_ge(prod_done, after + 1)
            nc.vector.tensor_tensor(L[:, 0], L[:, 0], mat(3 + 1), ALU.add).then_inc(mat_r, 1)
            tails(after + 1, 2, X[:, 2], after + 4)
            dve.wait_ge(mat_r, after + 4)
            link(nc.vector.tensor_tensor(L[:, 1], L[:, 0], X[:, 2], ALU.add))
            dve.wait_ge(prod_done, after + 2)
            nc.vector.tensor_tensor(L[:, 0], L[:, 1], mat(3 + 2), ALU.add).then_inc(mat_r, 1)
            dve.wait_ge(b_head, after + 3)
            nc.vector.tensor_tensor(b_s[:, 0, 1], L[:, 0], b_s[:, 0, 0], ALU.subtract).then_inc(split_r, 1)
            dve.wait_ge(eb_done, 1)
            nc.vector.tensor_tensor(eb2r[:, :], eb2[:, :], bank[6][0:NE, 0:D], ALU.add).then_inc(eb_r, 1)

            def expert_tails(e, par):
                dve.wait_ge(w_head, 2 * e + 2)
                nc.vector.tensor_tensor(w1_s[:, 1, bass.ds(e * (KC * FE), KC * FE)], w1_f[:, par],
                                        w1_s[:, 0, bass.ds(e * (KC * FE), KC * FE)], ALU.subtract)
                dve.wait_ge(w_head, 2 * e + 3)
                nc.vector.tensor_tensor(w2t_s[:, par, 1], w2t_f[:, par], w2t_s[:, par, 0], ALU.subtract)\
                    .then_inc(w_tail, 1)

            def folded(e, par):
                for h in range(2):
                    dve.wait_ge(fold_done, 2 * e + h + 1)
                    part = w2_f[:, par, h * 512:(h + 1) * 512]
                    nc.vector.tensor_tensor(part, part, bank[h][:, :], ALU.add).then_inc(w2_r, 1)
                dve.wait_ge(w2_head, e + 1)
                nc.vector.tensor_tensor(w2_s[:, 1, bass.ds(e * (FC * D), FC * D)], w2_f[:, par],
                                        w2_s[:, 0, bass.ds(e * (FC * D), FC * D)], ALU.subtract).then_inc(w2_tail, 1)

            for e in (0, 1):
                expert_tails(e, e)
                folded(e, e)
            with dve.Fori(2, NE - 1, 2) as e:
                for par in range(2):
                    expert_tails(e + par, par)
                    folded(e + par, par)

            def tokens(b, par):
                dve.wait_ge(xp_in, 16 * b + 16)
                for n in range(TT):
                    nc.vector.bn_stats(st[:, n], xp[:, par, n]).then_inc(st_r, 1)
                dve.wait_ge(st_r, TT * b + TT)
                dve.sem_inc(st_seen, 1)
                for n in range(TT):
                    nc.vector.bn_aggr(mv[:, n], st[:, n]).then_inc(mv_r, 1)
                dve.wait_ge(rs_r, b + 1)
                for n in range(TT):
                    nc.vector.tensor_scalar(z3[:, bass.ds(b * TT + n, 1)].rearrange("p a d -> p (a d)"), xp[:, par, n],
                                            mv[:, n, 0:1], rs[:, n:n + 1],
                                            ALU.subtract, ALU.mult).then_inc(z3_r, 1)
                dve.wait_ge(xn_r, 2 * b + 2)
                wait(dve, ab_done, 2 * b)
                nc.vector.tensor_copy(xn3_s[:, 0], xn3[:, :, :]).then_inc(xn_head, 1)
                dve.wait_ge(xn_head, b + 1)
                nc.vector.tensor_tensor(xn3_s[:, 1], xn3[:, :, :], xn3_s[:, 0], ALU.subtract).then_inc(xn_tail, 1)
                dve.wait_ge(lg_done, b + 1)
                nc.vector.tensor_tensor(of_tile(logits, b),
                                        bank[2][:, 0:TT * NE].rearrange("p (t e) -> p t e", t=TT),
                                        mgb[:, :].rearrange("p (a e) -> p a e", a=1).to_broadcast([P, TT, NE]),
                                        ALU.add).then_inc(lg_r, 1)
                for h in range(2):
                    dve.wait_ge(ab_done, 2 * b + h + 1)
                    wait(dve, ab_stored, 16 * b)
                    nc.vector.tensor_tensor(abel[:, 2 * h:2 * h + 2], pair(3 + h),
                                            abel_b[:, :].rearrange("p (a d) -> p a d", a=1).to_broadcast([P, 2, D]),
                                            ALU.add).then_inc(ab_r, 1)

            tokens(0, 0)
            tokens(1, 1)
            with dve.Fori(2, BATCHES - 1, 2) as b:
                tokens(b, 0)
                tokens(b + 1, 1)

            dve.wait_ge(lg_r, BATCHES)
            for n in range(NTILES):
                nc.vector.max(top[:, n], logits[:, n]).then_inc(top_r, 1)
            for n in range(NTILES):
                dve.wait_ge(top_r, n + 1)
                ins = nc.vector.max_index(topi[:, n], top[:, n], logits[:, n])
            link(ins)
            i0 = nc.vector.tensor_copy(topf[:, :, :].rearrange("p r n -> p n r"), topi[:, :, 0:2])
            nc.vector.tensor_tensor(td[:, :], top[:, :, 1], top[:, :, 0], ALU.subtract).then_inc(gap_r, 1)
            link(i0, nc.vector.tensor_copy(iota8[:, :], iota8i[:, :]),
                 nc.vector.tensor_copy(iota16[:, :], iota16i[:, :]),
                 nc.vector.tensor_copy(iotaq[:, :], iotaqi[:, :]))

            def over_e(x):
                return x.rearrange("p (n a) -> p n a", a=1).to_broadcast([P, NTILES, NE])

            def over_n(x):
                return x.rearrange("p (a e) -> p a e", a=1).to_broadcast([P, NTILES, NE])

            link(*[nc.vector.tensor_tensor(oh[:, r], over_n(iota8[:, :]), over_e(topf[:, r]), ALU.is_equal)
                   for r in range(2)],
                 nc.vector.tensor_scalar(iota16[:, :], iota16[:, :], float(SLOT), None, ALU.mult))
            nc.vector.tensor_tensor(picked[:, :, :], oh[:, 0], oh[:, 1], ALU.add).then_inc(picked_r, 1)
            dve.wait_ge(gap_exp, 1)
            link(nc.vector.tensor_scalar(wtop[:, 0], td[:, :], 1.0, None, ALU.add))
            link(nc.vector.reciprocal(wtop[:, 0], wtop[:, 0]))
            link(nc.vector.tensor_tensor(wtop[:, 1], td[:, :], wtop[:, 0], ALU.mult))
            link(nc.vector.tensor_tensor(wdense[:, :, :], oh[:, 0], over_e(wtop[:, 0]), ALU.mult),
                 nc.vector.tensor_tensor(prod[:, :, :], oh[:, 1], over_e(wtop[:, 1]), ALU.mult))
            dve.wait_ge(rank_done, 2)
            link(nc.vector.tensor_tensor(wdense[:, :, :], wdense[:, :, :], prod[:, :, :], ALU.add),
                 nc.vector.tensor_copy(tot[:, :, :], bank[6][:, 0:NTILES * NE].rearrange("p (n e) -> p n e", e=NE)))
            link(*[nc.vector.tensor_tensor_scan(cum[:, :, e], ones32[:, :], tot[:, :, e], 0.0, ALU.mult, ALU.add)
                   for e in range(NE)])
            link(nc.vector.tensor_tensor(slot[:, :, :], cum[:, :, :], tot[:, :, :], ALU.subtract),
                 nc.vector.tensor_tensor(
                     over[:, :, :],
                     cum[:, NTILES - 1, :].rearrange("p (e a) -> p e a", a=1).to_broadcast([P, NE, 16]),
                     iota16[:, :].rearrange("p (a m) -> p a m", a=1).to_broadcast([P, NE, 16]), ALU.is_gt))
            link(nc.vector.tensor_tensor(slot[:, :, :], slot[:, :, :],
                                         bank[5][:, 0:NTILES * NE].rearrange("p (n e) -> p n e", e=NE), ALU.add),
                 nc.vector.reduce_sum(ntile[:, :], over[:, :, :], AX.X))
            link(nc.vector.tensor_tensor_scan(cumt[:, :], ones32[:, 0:NE], ntile[:, :], 0.0, ALU.mult, ALU.add))
            link(nc.vector.tensor_tensor(base[:, :], cumt[:, :], ntile[:, :], ALU.subtract),
                 nc.vector.tensor_tensor(
                     below[:, :, :],
                     cumt[:, :].rearrange("p (a e) -> p a e", a=1).to_broadcast([P, QT, NE]),
                     iotaq[:, :].rearrange("p (q a) -> p q a", a=1).to_broadcast([P, QT, NE]), ALU.is_le))
            link(nc.vector.tensor_scalar(base[:, :], base[:, :], float(SLOT), None, ALU.mult),
                 nc.vector.reduce_sum(tef[:, :], below[:, :, :], AX.X))
            link(nc.vector.tensor_tensor(slot[:, :, :], slot[:, :, :], over_n(base[:, :]), ALU.add),
                 nc.vector.tensor_scalar(tef[:, :], tef[:, :], float(NE - 1), None, ALU.min))
            link(nc.vector.tensor_copy(tile_expert[:, :], tef[:, :]))
            for r in range(2):
                link(nc.vector.tensor_tensor(prod[:, :, :], slot[:, :, :], oh[:, r], ALU.mult))
                link(nc.vector.reduce_sum(posf[:, :], prod[:, :, :], AX.X))
                nc.vector.tensor_copy(pos[:, r], posf[:, :]).then_inc(pos_r, 1)
                dve.wait_ge(pos_r, r + 1)

        @block.tensor
        def _(pe):
            pe.wait_ge(const_done, 3)

            def turn(n, slot, src, need):
                pe.wait_ge(mat_r, need)
                for m in range(KC):
                    for k in range(KC):
                        last = nc.tensor.transpose(mat(slot)[:, k, m * P:(m + 1) * P],
                                                   src[:, m, k * P:(k + 1) * P], ident[:, :])
                last.then_inc(turned, 1)

            def product(n, slot):
                pe.wait_ge(split_r, n * 2 + 2)
                for m in range(KC):
                    last = split_product(nc, mat(3 + slot)[:, m], lambda s, k: aT_s[:, slot, s, k, m * P:(m + 1) * P],
                                         lambda s, k: b_s[:, slot, s, k], KC)
                last.then_inc(prod_done, 1)

            for r, src in enumerate((A, A2, L)):
                for s in range(GENS):
                    turn(r * GENS + s, s, src[:, s], r * GENS + s + 1)
                for s in range(GENS):
                    product(r * GENS + s, s)
            pe.wait_ge(sq_r, 4)
            squarings = pe.value_load(sq_i[0:1, 0:1], min_val=1, max_val=SQ_MAX)
            with pe.Fori(0, squarings) as k:
                for s in range(GENS):
                    turn(k * GENS + (3 * GENS + s), s, X[:, s], k * GENS + (3 * GENS + s + 1))
                for s in range(GENS):
                    product(k * GENS + (3 * GENS + s), s)
            after = squarings * GENS + 3 * GENS
            turn(after, 1, X[:, 0], after + 3)
            product(after, 1)
            turn(after + 1, 2, L[:, 0], after + 4)
            product(after + 1, 2)
            pe.wait_ge(split_r, after * 2 + 5)
            for k in range(KC):
                last = nc.tensor.matmul(bank[6][0:NE, 0:D], eb2t[:, k], L[:, 0, k], start=k == 0, stop=k == KC - 1)
            last.then_inc(eb_done, 1)

            def fold(e, par):
                pe.wait_ge(w_tail, e + 2)
                wait(pe, w2_r, 2 * e)
                for c in range(FC):
                    last = split_product(nc, pair(c // 2)[:, c % 2],
                                         lambda s, k: w2t_s[:, par, s, k * FE + c * P:k * FE + (c + 1) * P],
                                         lambda s, k: b_s[:, 0, s, k], KC)
                    if c % 2:
                        last.then_inc(fold_done, 1)

            for e in (0, 1):
                fold(e, e)
            with pe.Fori(2, NE - 1, 2) as e:
                for par in range(2):
                    fold(e + par, par)

            def tokens(b):
                pe.wait_ge(z3_r, TT * b + TT)
                if isinstance(b, int) and b == 0:
                    pe.wait_ge(w2_r, 2 * NE)
                wait(pe, xn_r, 2 * b)
                for c in range(KC):
                    for n in range(TT):
                        src = z3[:, bass.ds(b * TT + n, 1), c * P:(c + 1) * P].rearrange("p a d -> p (a d)") \
                            if not isinstance(b, int) else z3[:, b * TT + n, c * P:(c + 1) * P]
                        last = nc.tensor.transpose(bank[c][:, n * P:(n + 1) * P], zt(b, n, c), ident[:, :])
                    last.then_inc(zT_done, 1)
                pe.wait_ge(xn_r, 2 * b + 2)
                wait(pe, lg_r, b)
                for n in range(TT):
                    for k in range(KC):
                        last = nc.tensor.matmul(bank[2][:, n * NE:(n + 1) * NE], xn3[:, k, n * P:(n + 1) * P],
                                                mgw[:, k], start=k == 0, stop=k == KC - 1)
                last.then_inc(lg_done, 1)
                pe.wait_ge(xn_tail, b + 1)
                wait(pe, ab_r, 2 * b)
                for n in range(TT):
                    last = split_product(nc, pair(3 + n // 2)[:, n % 2],
                                         lambda s, k: xn3_s[:, s, k, n * P:(n + 1) * P],
                                         lambda s, k: abel_s[:, s, k], KC)
                    if n % 2:
                        last.then_inc(ab_done, 1)

            def zt(b, n, c):
                return z3[:, b * TT + n, c * P:(c + 1) * P]

            for b in range(BATCHES):
                tokens(b)
            pe.wait_ge(picked_r, 1)
            flat = picked[:, :, :].rearrange("p n e -> p (n e)")
            nc.tensor.matmul(bank[5][:, 0:NTILES * NE], tri[:, :], flat, start=True, stop=True).then_inc(rank_done, 1)
            nc.tensor.matmul(bank[6][:, 0:NTILES * NE], ones[:, :], flat, start=True, stop=True).then_inc(rank_done, 1)


def experts(nc, kept, zs_dram, ys_dram):
    ident, w1_s, w2_s, eb1, gamma, beta, tile_expert = [kept[n] for n in (
        "ident", "w1_s", "w2_s", "eb1", "gamma", "beta", "tile_expert")]
    ctx = ExitStack()
    with ctx:
        def sb(name, shape, dt=F32):
            return ctx.enter_context(nc.sbuf_tensor(name, shape, dt))

        def pb(name, shape, dt=F32):
            return ctx.enter_context(nc.psum_tensor(name, shape, dt))

        def sem(name):
            return ctx.enter_context(nc.semaphore(name))

        zs = sb("zs", [P, 2, ST, D])
        xe = sb("xe", [P, 2, KC, SLOT])
        xe_s = sb("xe_s", [P, 2, 2, KC, SLOT], BF16)
        hf = sb("hf_e", [P, 2, FC, SLOT])
        h_s = sb("h_s_e", [P, 2, 2, FC, SLOT], BF16)
        ye = sb("ye", [P, 2, ST, D])
        turn_bank = [pb(f"turn{i}", [P, KC, SLOT]) for i in range(2)]
        up_bank = [[pb(f"up{i}{j}", [P, 2, SLOT]) for j in range(2)] for i in range(2)]
        down_bank = [pb(f"down{i}", [P, ST, D]) for i in range(2)]
        zs_in = [sem("e_zs_in0"), sem("e_zs_in1")]
        ys_out = [sem("e_ys_out0"), sem("e_ys_out1")]
        turned, xe_r, xe_head, xe_tail, up_done, hf_r, h_head, h_tail, down_done, ye_r = [sem(n) for n in (
            "e_turned", "e_xe_r", "e_xe_head", "e_xe_tail", "e_up_done", "e_hf_r", "e_h_head", "e_h_tail",
            "e_down_done", "e_ye_r")]
        block = ctx.enter_context(nc.Block())

        def over_tiles(eng, body):
            body(0, 0)
            body(1, 1)
            with eng.Fori(2, QT - 1, 2) as q:
                body(q, 0)
                body(q + 1, 1)

        zs_v = zs_dram.rearrange("(q s p) d -> q p s d", s=ST, p=P)
        ys_v = ys_dram.rearrange("(q s p) d -> q p s d", s=ST, p=P)

        @block.sync
        def _(sp):
            def load(q, par):
                wait(sp, turned, q - 1)
                sp.dma_start(zs[:, par].rearrange("p s d -> p (s d)").rearrange("p (a s d) -> p a s d", a=1, s=ST),
                             zs_v[bass.ds(q, 1)].rearrange("a p s d -> p a s d")).then_inc(zs_in[par], 16)

            over_tiles(sp, load)

        @block.gpsimd
        def _(pool):
            def store(q, par):
                pool.wait_ge(ye_r, q + 1)
                pool.dma_start(ys_v[bass.ds(q, 1)].rearrange("a p s d -> p a s d"),
                               ye[:, par].rearrange("p s d -> p (s d)").rearrange("p (a s d) -> p a s d", a=1, s=ST))\
                    .then_inc(ys_out[par], 16)

            over_tiles(pool, store)
            for s in ys_out:
                pool.wait_ge(s, 16 * QT // 2)

        @block.scalar
        def _(act):
            def body(q, par):
                act.wait_ge(turned, q + 1)
                wait(act, xe_tail, q - 1)
                for c in range(KC):
                    nc.scalar.activation(xe[:, par, c], turn_bank[par][:, c], ACT.Identity, bias=beta[:, c:c + 1],
                                         scale=gamma[:, c:c + 1]).then_inc(xe_r, 1)
                e = act.value_load(tile_expert[0:1, bass.ds(q, 1)], min_val=0, max_val=NE - 1)
                for c in range(FC):
                    if c % 2 == 0:
                        act.wait_ge(up_done, 2 * q + c // 2 + 1)
                        wait(act, h_tail, q - 1)
                    nc.scalar.activation(hf[:, par, c], up_bank[par][c // 2][:, c % 2], ACT.Gelu,
                                         bias=eb1[:, bass.ds(e * FC + c, 1)]).then_inc(hf_r, 1)
                act.wait_ge(hf_r, FC * q + FC)
                wait(act, down_done, q - 1)
                nc.scalar.activation(h_s[:, par, 0], hf[:, par], ACT.Copy).then_inc(h_head, 1)

            over_tiles(act, body)

        @block.vector
        def _(dve):
            def body(q, par):
                dve.wait_ge(xe_r, KC * q + KC)
                wait(dve, up_done, 2 * (q - 1))
                nc.vector.tensor_copy(xe_s[:, par, 0], xe[:, par]).then_inc(xe_head, 1)
                dve.wait_ge(xe_head, q + 1)
                nc.vector.tensor_tensor(xe_s[:, par, 1], xe[:, par], xe_s[:, par, 0], ALU.subtract)\
                    .then_inc(xe_tail, 1)
                dve.wait_ge(h_head, q + 1)
                nc.vector.tensor_tensor(h_s[:, par, 1], hf[:, par], h_s[:, par, 0], ALU.subtract).then_inc(h_tail, 1)
                if isinstance(q, int):
                    if q:
                        results(q - 1, 1 - par)
                else:
                    results(q - 1, 1 - par)

            def results(q, par):
                dve.wait_ge(down_done, q + 1)
                if not (isinstance(q, int) and q < 2):
                    dve.wait_ge(ys_out[par], (q - par) * 8)
                nc.vector.tensor_copy(ye[:, par], down_bank[par][:, :, :]).then_inc(ye_r, 1)

            body(0, 0)
            body(1, 1)
            body(2, 0)
            body(3, 1)
            with dve.Fori(4, QT - 1, 2) as q:
                body(q, 0)
                body(q + 1, 1)
            results(QT - 1, 1)

        @block.tensor
        def _(pe):
            def turn(q, par):
                pe.wait_ge(zs_in[par], (q - par) * 8 + 16)
                wait(pe, xe_r, KC * (q - 1))
                for c in range(KC):
                    for s in range(ST):
                        last = nc.tensor.transpose(turn_bank[par][:, c, s * P:(s + 1) * P],
                                                   zs[:, par, s, c * P:(c + 1) * P], ident[:, :])
                last.then_inc(turned, 1)

            def up(q, par, e):
                pe.wait_ge(xe_tail, q + 1)
                for c in range(FC):
                    if c % 2 == 0:
                        wait(pe, hf_r, FC * (q - 2) + c + 2)
                    last = split_product(nc, up_bank[par][c // 2][:, c % 2],
                                         lambda s, k: w1_s[:, s, bass.ds(e * (KC * FE) + (k * FE + c * P), P)],
                                         lambda s, k: xe_s[:, par, s, k], KC)
                    if c % 2:
                        last.then_inc(up_done, 1)

            def down(q, par, e):
                pe.wait_ge(h_tail, q + 1)
                wait(pe, ye_r, q - 1)
                for n in range(ST):
                    last = split_product(nc, down_bank[par][:, n], lambda s, k: h_s[:, par, s, k, n * P:(n + 1) * P],
                                         lambda s, k: w2_s[:, s, bass.ds(e * (FC * D) + k * D, D)], FC)
                last.then_inc(down_done, 1)

            def expert_of(q):
                return pe.value_load(tile_expert[0:1, bass.ds(q, 1)], min_val=0, max_val=NE - 1)

            def body(q, par):
                turn(q + 1, 1 - par)
                up(q + 1, 1 - par, expert_of(q + 1))
                down(q, par, expert_of(q))

            turn(0, 0)
            up(0, 0, expert_of(0))
            body(0, 0)
            body(1, 1)
            body(2, 0)
            body(3, 1)
            with pe.Fori(4, QT - 3, 2) as q:
                body(q, 0)
                body(q + 1, 1)
            body(QT - 2, 0)
            down(QT - 1, 1, expert_of(QT - 1))


def combine(nc, kept, xp_dram, ab_dram, ys_dram, out):
    ident, eb2r, gc1_row, gc2_row, gc_b, neg_half, eps_t, wdense, wtop, pos = [kept[n] for n in (
        "ident", "eb2r", "gc1_row", "gc2_row", "gc_b", "neg_half", "eps_t", "wdense", "wtop", "pos")]
    ctx = ExitStack()
    with ctx:
        def sb(name, shape, dt=F32):
            return ctx.enter_context(nc.sbuf_tensor(name, shape, dt))

        def pb(name, shape, dt=F32):
            return ctx.enter_context(nc.psum_tensor(name, shape, dt))

        def sem(name):
            return ctx.enter_context(nc.semaphore(name))

        bank = [pb(f"cbank{k}", [P, 512]) for k in range(4)]
        got = sb("got", [P, 2, 2, TT, D])
        abel = sb("abel_c", [P, 2, TT, D])
        xp = sb("xp_c", [P, 2, TT, D])
        wdT = sb("wdT", [NE, TT, P])
        moe = sb("moe", [P, TT, D])
        t1, t2 = sb("t1", [P, TT, D]), sb("t2", [P, TT, D])
        s1, s2, gate = sb("s1", [P, TT]), sb("s2", [P, TT]), sb("gate_c", [P, TT])
        st, mv, rs = sb("st_c", [P, TT, 6]), sb("mv_c", [P, TT, 2]), sb("rs_c", [P, TT])
        res = sb("res", [P, TT, D])
        got_in = [sem("c_got0"), sem("c_got1")]
        ab_in, wdT_done, wdT_r, bias_done, step, ls_r, gate_r, mv_r, ve_r, rs_r, res_r, stored, blk = [
            sem(n) for n in ("c_ab_in", "c_wdT_done", "c_wdT_r", "c_bias_done", "c_step", "c_ls_r", "c_gate_r",
                             "c_mv_r", "c_ve_r", "c_rs_r", "c_res_r", "c_stored", "c_blk")]
        block = ctx.enter_context(nc.Block())

        def rows_of(dram, b):
            return dram[b].rearrange("(t p) d -> p t d", p=P)

        @block.sync
        def _(sp):
            def load(b):
                wait(sp, res_r, TT * (b - 1))
                wait(sp, ab_in, 32 * b)
                sp.dma_start(abel[:, b % 2], rows_of(ab_dram, b)).then_inc(ab_in, 16)
                sp.dma_start(xp[:, b % 2], rows_of(xp_dram, b)).then_inc(ab_in, 16)

            load(0)
            for b in range(BATCHES):
                if b + 1 < BATCHES:
                    load(b + 1)
                sp.wait_ge(res_r, TT * (b + 1))
                sp.dma_start(rows_of(out, b), res[:, :, :]).then_inc(stored, 16)
            sp.wait_ge(stored, 16 * BATCHES)

        @block.gpsimd
        def _(pool):
            def gather(b):
                wait(pool, ls_r, 2 * (b - 1))
                for r in range(2):
                    for n in range(TT):
                        nc.gpsimd.indirect_dma_start(
                            out=got[:, b % 2, r, n, :], out_offset=None, in_=ys_dram[:, :],
                            in_offset=bass.IndirectOffsetOnAxis(ap=pos[:, r, b * TT + n:b * TT + n + 1], axis=0))\
                            .then_inc(got_in[b % 2], 16)

            gather(0)
            for b in range(BATCHES):
                if b + 1 < BATCHES:
                    gather(b + 1)
                pool.wait_ge(mv_r, TT * b + TT)
                nc.gpsimd.tensor_tensor(rs[:, :], mv[:, :, 1], eps_t[:, :], ALU.add).then_inc(ve_r, 1)
                pool.wait_ge(ve_r, b + 1)
                nc.gpsimd.tensor_tensor(rs[:, :], rs[:, :], neg_half[:, :], ALU.pow).then_inc(rs_r, 1)

        @block.scalar
        def _(act):
            for b in range(BATCHES):
                act.wait_ge(wdT_done, b + 1)
                wait(act, bias_done, b)
                nc.scalar.activation(wdT[:, :, :].rearrange("e t p -> e (t p)"), bank[2 + b % 2][0:NE, :], ACT.Copy)\
                    .then_inc(wdT_r, 1)
                act.wait_ge(ls_r, 2 * b + 2)
                nc.scalar.activation(gate[:, :], s2[:, :], ACT.Sigmoid, bias=gc_b[:, :]).then_inc(gate_r, 1)

        @block.tensor
        def _(pe):
            for b in range(BATCHES):
                wait(pe, wdT_r, b - 1)
                for n in range(TT):
                    last = nc.tensor.transpose(bank[2 + b % 2][0:NE, n * P:(n + 1) * P], wdense[:, b * TT + n, :],
                                               ident[:, :])
                last.then_inc(wdT_done, 1)
                pe.wait_ge(wdT_r, b + 1)
                wait(pe, blk, b)
                for n in range(TT):
                    last = nc.tensor.matmul(bank[n // 2][:, (n % 2) * D:(n % 2 + 1) * D], wdT[:, n], eb2r[:, :],
                                            start=True, stop=True)
                last.then_inc(bias_done, 1)

        @block.vector
        def _(dve):
            links = [0]

            def link(*ins):
                for i in ins:
                    i.then_inc(step, 1)
                links[0] += len(ins)
                dve.wait_ge(step, links[0])

            def over_d(row):
                return row[:, :].rearrange("p (a d) -> p a d", a=1).to_broadcast([P, TT, D])

            for b in range(BATCHES):
                par = b % 2
                dve.wait_ge(ab_in, 32 * (b + 1))
                link(nc.vector.tensor_tensor(t1[:, :, :], abel[:, par], over_d(gc1_row), ALU.mult))
                link(nc.vector.reduce_sum(s1[:, :], t1[:, :, :], AX.X))
                dve.wait_ge(bias_done, b + 1)
                dve.wait_ge(got_in[par], 16 * 2 * TT * (b // 2 + 1))
                link(*[nc.vector.scalar_tensor_tensor(moe[:, n], got[:, par, 0, n], wtop[:, 0, b * TT + n:b * TT + n + 1],
                                                      bank[n // 2][:, (n % 2) * D:(n % 2 + 1) * D], ALU.mult, ALU.add)
                       for n in range(TT)])
                for n in range(TT):
                    last = nc.vector.scalar_tensor_tensor(moe[:, n], got[:, par, 1, n],
                                                          wtop[:, 1, b * TT + n:b * TT + n + 1],
                                                          moe[:, n], ALU.mult, ALU.add)
                    link(last)
                link(nc.vector.tensor_tensor(t2[:, :, :], moe[:, :, :], over_d(gc2_row), ALU.mult))
                nc.vector.reduce_sum(s2[:, :], t2[:, :, :], AX.X).then_inc(ls_r, 1)
                dve.wait_ge(ls_r, 2 * b + 1)
                nc.vector.tensor_tensor(s2[:, :], s1[:, :], s2[:, :], ALU.add).then_inc(ls_r, 1)
                link(nc.vector.tensor_tensor(moe[:, :, :], moe[:, :, :], abel[:, par], ALU.subtract))
                nc.vector.tensor_scalar(s1[:, :], s1[:, :], 1.0, None, ALU.mult).then_inc(blk, 1)
                dve.wait_ge(gate_r, b + 1)
                link(*[nc.vector.scalar_tensor_tensor(moe[:, n], moe[:, n], gate[:, n:n + 1], abel[:, par, n],
                                                      ALU.mult, ALU.add) for n in range(TT)])
                link(nc.vector.scalar_tensor_tensor(moe[:, :, :], xp[:, par], 2.0, moe[:, :, :], ALU.mult, ALU.add))
                link(*[nc.vector.bn_stats(st[:, n], moe[:, n]) for n in range(TT)])
                for n in range(TT):
                    nc.vector.bn_aggr(mv[:, n], st[:, n]).then_inc(mv_r, 1)
                dve.wait_ge(rs_r, b + 1)
                wait(dve, stored, 16 * b)
                for n in range(TT):
                    nc.vector.tensor_scalar(res[:, n], moe[:, n], mv[:, n, 0:1], rs[:, n:n + 1],
                                            ALU.subtract, ALU.mult).then_inc(res_r, 1)


def build(nc, t, out, scratch):
    mamba_half(nc, t, scratch["xp"])
    moe_half(nc, t, scratch["xp"], scratch["abel"], scratch["zs"], scratch["ys"], out)


def kernel(**inputs):
    import numpy as _np
    import concourse.bacc as _bacc
    from concourse import mybir as _mybir
    from concourse.bass_utils import run_bass_kernel_spmd as _run

    a = {k: _np.ascontiguousarray(v) for k, v in inputs.items()}

    def columns(x):
        return x.reshape(-1, P).T

    def rows(x):
        return _np.broadcast_to(x.reshape(1, -1), (P, x.size))

    L, F = "L0_attn_", "L0_ffn_"
    laid = {
        "x": a[L + "x"], "n1w": columns(a[L + "norm1_w"]), "n1b": columns(a[L + "norm1_b"]),
        "n2w": columns(a[L + "norm2_w"]), "n2b": columns(a[L + "norm2_b"]),
        "gate_b": columns(a[L + "gate_b"]), "state_b": columns(a[L + "state_b"]),
        "mlp_b1": columns(a[L + "mlp_b1"]), "out_b_row": rows(a[L + "out_b"]),
        "mlp_b2_row": rows(a[L + "mlp_b2"]), "state_b_row": rows(a[L + "state_b"]),
        "gate_w": a[L + "gate_w"], "state_w": a[L + "state_w"], "out_w": a[L + "out_w"],
        "mlp_w1": a[L + "mlp_w1"], "mlp_w2": a[L + "mlp_w2"],
        "gamma": columns(a[F + "ln_gamma"]), "beta": columns(a[F + "ln_beta"]),
        "abel_w": a[F + "abel_w"], "abel_b": rows(a[F + "abel_b"]),
        "mgw": a[F + "moe_gate_w"], "mgb": rows(a[F + "moe_gate_b"]),
        "ew1": a[F + "ew1"], "eb1": columns(a[F + "eb1"]),
        "ew2": a[F + "ew2"], "ew2t": a[F + "ew2"].transpose(0, 2, 1),
        "eb2": a[F + "eb2"], "eb2t": a[F + "eb2"].T, "gens": a[F + "gens"],
        "gc1_row": rows(a[F + "gc_w"][:D]), "gc2_row": rows(a[F + "gc_w"][D:]), "gc_b": rows(a[F + "gc_b"]),
    }
    nc = _bacc.Bacc("TRN2", target_bir_lowering=False, num_devices=1)
    arrays, t = {}, {}
    for name, x in laid.items():
        x = _np.ascontiguousarray(x)
        arrays["in_" + name] = x
        t[name] = nc.dram_tensor("in_" + name, x.shape, _mybir.dt.from_np(x.dtype), kind="ExternalInput").ap()
    out = nc.dram_tensor("out_0", (BATCHES, TOKENS, D), F32, kind="ExternalOutput").ap()
    scratch = {name: nc.dram_tensor("scratch_" + name, shape, F32, kind="Internal").ap() for name, shape in (
        ("xp", (BATCHES, TOKENS, D)), ("abel", (BATCHES, TOKENS, D)),
        ("zs", (QT * SLOT, D)), ("ys", (QT * SLOT, D)))}
    build(nc, t, out, scratch)
    r = _run(nc, [arrays], core_ids=[0])
    return r.results[0]["out_0"]
```

```python
import concourse.bass as bass
from concourse import mybir
from contextlib import ExitStack


F32 = mybir.dt.float32
BF16 = mybir.dt.bfloat16
I32 = mybir.dt.int32
U32 = mybir.dt.uint32
ALU = mybir.AluOpType
ACT = mybir.ActivationFunctionType
AX = mybir.AxisListType

P = 128
BATCHES, TOKENS, D = 8, 512, 256
KC = D // P
TT = TOKENS // P
HID = 1024
HC = HID // P
EPS = 1e-5
NE, FE = 8, 512
FC = FE // P
NTILES = BATCHES * TT
SLOT = 256
ST = SLOT // P
QT = (2 * NTILES * P // SLOT + NE - 1 + 1) // 2 * 2
ROW = D + 1
NOWHERE = 1 << 20
FILL = 4
FILLS = QT * SLOT // (P * FILL)


def wait(eng, sem, value):
    if not isinstance(value, int) or value > 0:
        eng.wait_ge(sem, value)


def split_product(nc, dst, lhs, rhs, terms, start=True, stop=True):
    n, last = 0, None
    total = 3 * terms
    for k in range(terms):
        for a, b in ((0, 0), (0, 1), (1, 0)):
            last = nc.tensor.matmul(dst, lhs(a, k), rhs(b, k), start=start and n == 0,
                                    stop=stop and n == total - 1)
            n += 1
    return last



def mamba_half(nc, t, xp_dram, zs_dram):
    ctx = ExitStack()
    with ctx:
        def sb(name, shape, dt=F32):
            return ctx.enter_context(nc.sbuf_tensor(name, shape, dt))

        def pb(name, shape, dt=F32):
            return ctx.enter_context(nc.psum_tensor(name, shape, dt))

        used = []

        def sem(name):
            used.append(ctx.enter_context(nc.semaphore(name)))
            return used[-1]

        ident = sb("ident", [P, P])
        neg_half = sb("neg_half", [P, TT])
        eps_t = sb("eps_t", [P, TT])
        n1w, n1b = sb("n1w", [P, KC]), sb("n1b", [P, KC])
        n2w, n2b = sb("n2w", [P, KC]), sb("n2b", [P, KC])
        gate_b = sb("gate_b", [P, 2 * KC])
        state_b = sb("state_b", [P, KC])
        mlp_b1 = sb("mlp_b1", [P, HC])
        out_b_row = sb("out_b_row", [P, D])
        mlp_b2_row = sb("mlp_b2_row", [P, D])
        state_b_row = sb("state_b_row", [P, D])
        vectors = [(n1w, "n1w"), (n1b, "n1b"), (n2w, "n2w"), (n2b, "n2b"), (gate_b, "gate_b"),
                   (state_b, "state_b"), (mlp_b1, "mlp_b1"), (out_b_row, "out_b_row"),
                   (mlp_b2_row, "mlp_b2_row"), (state_b_row, "state_b_row")]
        gate_w = sb("gate_w", [P, 2, KC, 2 * D], BF16)
        state_w = sb("state_w", [P, 2, KC, D], BF16)
        mean_w = sb("mean_w", [P, 2, KC, P], BF16)
        out_w = sb("out_w", [P, 2, KC, D], BF16)
        mlp_w1 = sb("mlp_w1", [P, 2, KC, HID], BF16)
        mlp_w2 = sb("mlp_w2", [P, 2, HC, D], BF16)
        weights = [(gate_w, "gate_w", KC, 2 * D), (state_w, "state_w", KC, D), (out_w, "out_w", KC, D),
                   (mlp_w1, "mlp_w1", KC, HID), (mlp_w2, "mlp_w2", HC, D)]
        fill = sb("fill", [P, FILL, ROW])
        staged = sb("staged", [P, 2, 2048])
        mean_col = sb("mean_col", [P, KC])
        mean_full = sb("mean_full", [P, KC, P])
        mean_b = sb("mean_b", [P, 1])

        x_in = sb("x_in", [P, 2, TT, D])
        x_ob = sb("x_ob", [P, TT, D])
        x_b2 = sb("x_b2", [P, TT, D])
        x_res = sb("x_res", [P, TT, D])
        st1, mv1, rs1 = sb("st1", [P, TT, 6]), sb("mv1", [P, TT, 2]), sb("rs1", [P, TT])
        st2, mv2, rs2 = sb("st2", [P, TT, 6]), sb("mv2", [P, TT, 2]), sb("rs2", [P, TT])
        st3, mv3, rs3 = sb("st3", [P, TT, 6]), sb("mv3", [P, TT, 2]), sb("rs3", [P, TT])
        z1 = sb("z1", [P, TT, D])
        xn = sb("xn", [P, KC, TOKENS])
        xn_s = sb("xn_s", [P, 2, KC, TOKENS], BF16)
        g = sb("g", [P, KC, TOKENS])
        gg = sb("gg", [P, KC, TOKENS])
        g_s = sb("g_s", [P, 2, KC, TOKENS], BF16)
        gg_s = sb("gg_s", [P, 2, KC, TOKENS], BF16)
        az = sb("az", [P, TOKENS])
        rz = sb("rz", [P, TOKENS])
        delta = sb("delta", [P, TOKENS])
        decay = sb("decay", [P, TOKENS])
        u = sb("u", [P, KC, TOKENS])
        q = sb("q", [P, KC, TOKENS])
        y = sb("y", [P, KC, TOKENS])
        y_s = sb("y_s", [P, 2, KC, TOKENS], BF16)
        x1 = sb("x1", [P, TT, D])
        z2 = sb("z2", [P, TT, D])
        xn2 = sb("xn2", [P, KC, TOKENS])
        xn2_s = sb("xn2_s", [P, 2, KC, TOKENS], BF16)
        HR = 4
        hf = sb("hf", [P, HR, TOKENS])
        h_s = sb("h_s", [P, 2, HC, TOKENS], BF16)
        v = sb("v", [P, TT, D])
        xp = sb("xp", [P, TT, D])

        bank = [pb(f"bank{k}", [P, 512]) for k in range(8)]

        def token_pair(k):
            return bank[k][:, :].rearrange("p (t d) -> p t d", t=2)

        vec_in, w_head, w_tail = sem("vec_in"), sem("w_head"), sem("w_tail")
        w_in = [sem("w_in_even"), sem("w_in_odd")]
        mean_done, ident_done = sem("mean_done"), sem("ident_done")
        x_loaded, x_used = sem("x_loaded"), sem("x_used")
        st1_r, mv1_r, ve1_r, rs1_r, z1_r = [sem(n) for n in ("st1_r", "mv1_r", "ve1_r", "rs1_r", "z1_r")]
        st2_r, mv2_r, ve2_r, rs2_r, z2_r = [sem(n) for n in ("st2_r", "mv2_r", "ve2_r", "rs2_r", "z2_r")]
        st3_r, mv3_r, ve3_r, rs3_r, xp_r = [sem(n) for n in ("st3_r", "mv3_r", "ve3_r", "rs3_r", "xp_r")]
        zT_done, xn_r, xn_head, xn_tail = [sem(n) for n in ("zT_done", "xn_r", "xn_head", "xn_tail")]
        gate_done, g_r, xg_r, g_head, g_tail, gg_head, gg_tail = [sem(n) for n in (
            "gate_done", "g_r", "xg_r", "g_head", "g_tail", "gg_head", "gg_tail")]
        zz_done, az_r, rz_r, ez_r, lz_r, delta_r, decay_r = [sem(n) for n in (
            "zz_done", "az_r", "rz_r", "ez_r", "lz_r", "delta_r", "decay_r")]
        u_done, b_done, u_r, q_r, dq_r, y_r, y_head, y_tail = [sem(n) for n in (
            "u_done", "b_done", "u_r", "q_r", "dq_r", "y_r", "y_head", "y_tail")]
        out_done, xob_r, xb2_r, x1_r, xres_r = [sem(n) for n in ("out_done", "xob_r", "xb2_r", "x1_r", "xres_r")]
        z2T_done, xn2_r, xn2_head, xn2_tail = [sem(n) for n in ("z2T_done", "xn2_r", "xn2_head", "xn2_tail")]
        m_done, hf_r, h_head, h_tail, o_done, v_r = [sem(n) for n in (
            "m_done", "hf_r", "h_head", "h_tail", "o_done", "v_r")]
        fill_r, zs_filled = sem("fill_r"), sem("zs_filled")
        xp_stored, st_seen = sem("xp_stored"), sem("st_seen")

        LAST = BATCHES - 1
        LOOP0, LOOP1 = 2, 6

        def over_batches(eng, first, step, last):
            first()
            step(0, 0)
            step(1, 1)
            with eng.Fori(LOOP0, LOOP1, 2) as i:
                step(i, 0)
                step(i + 1, 1)
            step(LAST - 1, (LAST - 1) % 2)
            step(LAST, LAST % 2)
            last()

        def is_first(i):
            return isinstance(i, int) and i == 0

        def is_last(i):
            return isinstance(i, int) and i == LAST

        block = ctx.enter_context(nc.Block())

        @block.sync
        def _(sp):
            for tile, name in vectors:
                sp.dma_start(tile[:, :], t[name]).then_inc(vec_in, 16)

            def load_x(i, par):
                wait(sp, x_used, i - 1)
                wait(sp, x_loaded, 16 * i)
                sp.dma_start(x_in[:, par], t["x"][bass.ds(i, 1)].rearrange("b (t p) d -> p (b t) d", p=P))\
                    .then_inc(x_loaded, 16)

            load_x(0, 0)
            for n, (_, name, k, width) in enumerate(weights):
                wait(sp, w_tail, n - 1)
                sp.dma_start(staged[:, n % 2, 0:k * width].rearrange("p (k n) -> p k n", k=k),
                             t[name].rearrange("(k p) n -> p k n", p=P)).then_inc(w_in[n % 2], 16)

            sp.wait_ge(fill_r, 2)
            zv = zs_dram.rearrange("(a p c) d -> a p c d", p=P, c=FILL)
            for a in range(FILLS):
                sp.dma_start(zv[a], fill[:, :, :]).then_inc(zs_filled, 16)

            def step(i, par):
                if not is_last(i):
                    load_x(i + 1, 1 - par)
                if not is_first(i):
                    store_xp(i - 1)

            def store_xp(j):
                sp.wait_ge(xp_r, 4 * j + 4)
                sp.dma_start(xp_dram[bass.ds(j, 1)].rearrange("b (t p) d -> p (b t) d", p=P), xp[:, :, :]).then_inc(xp_stored, 16)

            over_batches(sp, lambda: None, step, lambda: store_xp(LAST))
            sp.wait_ge(xp_stored, 16 * BATCHES)
            sp.wait_ge(zs_filled, 16 * FILLS)
            sp.wait_ge(st_seen, 3 * BATCHES)

        @block.gpsimd
        def _(pool):
            nc.gpsimd.memset(ident[:, :], 0.0).then_inc(ident_done, 1)
            nc.gpsimd.memset(neg_half[:, :], -0.5)
            nc.gpsimd.memset(eps_t[:, :], EPS).then_inc(ident_done, 1)
            pool.wait_ge(ident_done, 2)
            nc.gpsimd.affine_select(out=ident[:, :], in_=ident[:, :], compare_op=ALU.not_equal, fill=1.0,
                                    base=0, pattern=[[-1, P]], channel_multiplier=1).then_inc(ident_done, 1)
            nc.gpsimd.memset(fill[:, :, :], 0.0).then_inc(fill_r, 1)
            pool.wait_ge(fill_r, 1)
            nc.gpsimd.memset(fill[:, :, D:ROW].bitcast(I32), NOWHERE).then_inc(fill_r, 1)
            pool.wait_ge(vec_in, 16 * len(vectors))

            def rstd(mv, ve_r, rs, rs_r, mv_r, b):
                pool.wait_ge(mv_r, TT * b + TT)
                nc.gpsimd.tensor_tensor(rs[:, :], mv[:, :, 1], eps_t[:, :], ALU.add).then_inc(ve_r, 1)
                pool.wait_ge(ve_r, b + 1)
                nc.gpsimd.tensor_tensor(rs[:, :], rs[:, :], neg_half[:, :], ALU.pow).then_inc(rs_r, 1)

            def bias_rows(i, par):
                pool.wait_ge(x_loaded, 16 * i + 16)
                wait(pool, x1_r, 2 * i)
                nc.gpsimd.tensor_tensor(x_ob[:, :, :], x_in[:, par], row4(out_b_row), ALU.add).then_inc(xob_r, 1)
                nc.gpsimd.tensor_tensor(x_b2[:, :, :], x_in[:, par], row4(mlp_b2_row), ALU.add).then_inc(xb2_r, 1)
                pool.wait_ge(xb2_r, i + 1)
                pool.wait_ge(xob_r, i + 1)
                pool.wait_ge(z1_r, TT * i + TT)
                pool.sem_inc(x_used, 1)

            def row4(row):
                return row[:, :].rearrange("p (a d) -> p a d", a=1).to_broadcast([P, TT, D])

            def residual(j):
                pool.wait_ge(x1_r, 2 * j + 2)
                pool.wait_ge(xb2_r, j + 1)
                wait(pool, v_r, 2 * j)
                nc.gpsimd.tensor_tensor(x_res[:, :, :], x1[:, :, :], x_b2[:, :, :], ALU.add).then_inc(xres_r, 1)
                pool.wait_ge(xres_r, j + 1)

            def step(i, par):
                if not is_first(i):
                    residual(i - 1)
                bias_rows(i, par)
                if not is_last(i):
                    rstd(mv1, ve1_r, rs1, rs1_r, mv1_r, i + 1)
                if not is_first(i):
                    rstd(mv3, ve3_r, rs3, rs3_r, mv3_r, i - 1)
                rstd(mv2, ve2_r, rs2, rs2_r, mv2_r, i)

            def last():
                residual(LAST)
                rstd(mv3, ve3_r, rs3, rs3_r, mv3_r, LAST)

            over_batches(pool, lambda: rstd(mv1, ve1_r, rs1, rs1_r, mv1_r, 0), step, last)

        @block.scalar
        def _(act):
            for n, (tile, _, k, width) in enumerate(weights):
                act.wait_ge(w_in[n % 2], 16 * (n // 2) + 16)
                nc.scalar.activation(tile[:, 0], staged[:, n % 2, 0:k * width].rearrange("p (k n) -> p k n", k=k),
                                     ACT.Copy).then_inc(w_head, 1)
            act.wait_ge(vec_in, 16 * len(vectors))
            act.wait_ge(mean_done, 5)

            def norm1(i):
                for c in range(KC):
                    act.wait_ge(zT_done, 2 * i + c + 1)
                    wait(act, xg_r, i)
                    wait(act, xn_tail, i)
                    nc.scalar.activation(xn[:, c], bank[c][:, :], ACT.Identity, bias=n1b[:, c:c + 1],
                                         scale=n1w[:, c:c + 1]).then_inc(xn_r, 1)

            def silus(i):
                for c in range(2 * KC):
                    act.wait_ge(gate_done, 4 * i + c + 1)
                    wait(act, g_tail if c < KC else gg_tail, i)
                    dst = g if c < KC else gg
                    nc.scalar.activation(dst[:, c % KC], bank[c][:, :], ACT.Silu,
                                         bias=gate_b[:, c:c + 1]).then_inc(g_r, 1)
                act.wait_ge(g_r, 4 * i + 4)
                wait(act, b_done, 2 * i)
                nc.scalar.activation(gg_s[:, 0], gg[:, :, :], ACT.Copy).then_inc(gg_head, 1)

            def norm2(j):
                for c in range(KC):
                    act.wait_ge(z2T_done, 2 * j + c + 1)
                    wait(act, xn2_tail, j)
                    nc.scalar.activation(xn2[:, c], bank[5 + c][:, :], ACT.Identity, bias=n2b[:, c:c + 1],
                                         scale=n2w[:, c:c + 1]).then_inc(xn2_r, 1)

            def magnitudes(i):
                act.wait_ge(zz_done, i + 1)
                wait(act, delta_r, i)
                nc.scalar.activation(az[:, :], bank[4][:, :], ACT.Abs, bias=mean_b[:, :]).then_inc(az_r, 1)
                nc.scalar.activation(rz[:, :], bank[4][:, :], ACT.Relu, bias=mean_b[:, :]).then_inc(rz_r, 1)

            def decays(i):
                nc.scalar.preload_act_table_set("natural_log_exp_and_others")
                act.wait_ge(az_r, i + 1)
                nc.scalar.activation(az[:, :], az[:, :], ACT.Exp, scale=-1.0).then_inc(ez_r, 1)
                act.wait_ge(ez_r, i + 1)
                nc.scalar.activation(az[:, :], az[:, :], ACT.Ln, bias=1.0).then_inc(lz_r, 1)
                act.wait_ge(delta_r, i + 1)
                wait(act, y_r, 2 * i)
                nc.scalar.activation(decay[:, :], delta[:, :], ACT.Exp, scale=-1.0).then_inc(decay_r, 1)

            def gelus(j):
                for k in range(HC):
                    act.wait_ge(m_done, HC * j + k + 1)
                    wait(act, h_tail, HC * j + k + 1 - HR)
                    nc.scalar.activation(hf[:, k % HR], bank[5 + (2 + k) % 3][:, :], ACT.Gelu,
                                         bias=mlp_b1[:, k:k + 1]).then_inc(hf_r, 1)
                    act.wait_ge(hf_r, HC * j + k + 1)
                    nc.scalar.activation(h_s[:, 0, k], hf[:, k % HR], ACT.Copy).then_inc(h_head, 1)

            def us(i):
                for c in range(KC):
                    act.wait_ge(u_done, 2 * i + c + 1)
                    wait(act, q_r, 2 * i)
                    nc.scalar.activation(u[:, c], bank[c][:, :], ACT.Identity,
                                         bias=state_b[:, c:c + 1]).then_inc(u_r, 1)

            def y_heads(i):
                act.wait_ge(y_r, 2 * i + 2)
                wait(act, out_done, 2 * i)
                nc.scalar.activation(y_s[:, 0], y[:, :, :], ACT.Copy).then_inc(y_head, 1)

            def step(i, par):
                silus(i)
                if not is_first(i):
                    norm2(i - 1)
                magnitudes(i)
                if not is_first(i):
                    gelus(i - 1)
                decays(i)
                us(i)
                if not is_last(i):
                    norm1(i + 1)
                y_heads(i)

            def last():
                norm2(LAST)
                gelus(LAST)

            over_batches(act, lambda: norm1(0), step, last)

        @block.vector
        def _(dve):
            dve.wait_ge(vec_in, 16 * len(vectors))
            nc.vector.reduce_sum(mean_b[:, :], state_b_row[:, :], AX.X).then_inc(mean_done, 1)
            dve.wait_ge(mean_done, 1)
            nc.vector.tensor_scalar(mean_b[:, :], mean_b[:, :], 1.0 / D, None, ALU.mult).then_inc(mean_done, 1)
            for n, (tile, name, k, width) in enumerate(weights):
                src = staged[:, n % 2, 0:k * width].rearrange("p (k n) -> p k n", k=k)
                if name == "state_w":
                    dve.wait_ge(w_in[n % 2], 16 * (n // 2) + 16)
                    nc.vector.reduce_sum(mean_col[:, :], src, AX.X).then_inc(mean_done, 1)
                dve.wait_ge(w_head, n + 1)
                nc.vector.tensor_tensor(tile[:, 1], src, tile[:, 0], ALU.subtract).then_inc(w_tail, 1)
            dve.wait_ge(mean_done, 3)
            nc.vector.tensor_scalar(mean_full[:, :, :],
                                    mean_col[:, :].rearrange("p (k a) -> p k a", a=1).to_broadcast([P, KC, P]),
                                    1.0 / D, None, ALU.mult).then_inc(mean_done, 1)
            dve.wait_ge(mean_done, 4)
            nc.vector.tensor_copy(mean_w[:, 0], mean_full[:, :, :]).then_inc(mean_done, 1)
            dve.wait_ge(mean_done, 5)
            nc.vector.tensor_tensor(mean_w[:, 1], mean_full[:, :, :], mean_w[:, 0], ALU.subtract)\
                .then_inc(mean_done, 1)

            def stats(src, st, st_r, mv, mv_r, b, free):
                for n in range(TT):
                    nc.vector.bn_stats(st[:, n], src[:, n]).then_inc(st_r, 1)
                dve.wait_ge(st_r, TT * b + TT)
                dve.sem_inc(st_seen, 1)
                for n in range(TT):
                    nc.vector.bn_aggr(mv[:, n], st[:, n]).then_inc(mv_r, 1)

            def normalise(dst, src, mv, rs, rs_r, done, b):
                dve.wait_ge(rs_r, b + 1)
                for n in range(TT):
                    nc.vector.tensor_scalar(dst[:, n], src[:, n], mv[:, n, 0:1], rs[:, n:n + 1],
                                            ALU.subtract, ALU.mult).then_inc(done, 1)

            def split(dst, src, head, tail, b):
                nc.vector.tensor_copy(dst[:, 0], src).then_inc(head, 1)
                dve.wait_ge(head, b + 1)
                nc.vector.tensor_tensor(dst[:, 1], src, dst[:, 0], ALU.subtract).then_inc(tail, 1)

            def norm1(i, par):
                dve.wait_ge(x_loaded, 16 * i + 16)
                wait(dve, rs1_r, i)
                stats(x_in[:, par], st1, st1_r, mv1, mv1_r, i, None)
                wait(dve, zT_done, 2 * i)
                normalise(z1, x_in[:, par], mv1, rs1, rs1_r, z1_r, i)

            def norm1_split(i):
                dve.wait_ge(xn_r, 2 * i + 2)
                wait(dve, zz_done, i)
                split(xn_s, xn[:, :, :], xn_head, xn_tail, i)

            def norm2(j):
                for h in range(2):
                    dve.wait_ge(out_done, 2 * j + h + 1)
                    dve.wait_ge(xob_r, j + 1)
                    wait(dve, xres_r, j)
                    nc.vector.tensor_tensor(x1[:, 2 * h:2 * h + 2], token_pair(2 + h), x_ob[:, 2 * h:2 * h + 2],
                                            ALU.add).then_inc(x1_r, 1)
                dve.wait_ge(x1_r, 2 * j + 2)
                stats(x1, st2, st2_r, mv2, mv2_r, j, None)

            def norm2_rows(j):
                wait(dve, z2T_done, 2 * j)
                normalise(z2, x1, mv2, rs2, rs2_r, z2_r, j)

            def norm2_split(j):
                dve.wait_ge(xn2_r, 2 * j + 2)
                wait(dve, m_done, HC * j)
                split(xn2_s, xn2[:, :, :], xn2_head, xn2_tail, j)

            def gates(i):
                dve.wait_ge(g_r, 4 * i + 2)
                nc.vector.tensor_tensor(g[:, :, :], g[:, :, :], xn[:, :, :], ALU.mult).then_inc(xg_r, 1)
                dve.wait_ge(xg_r, i + 1)
                wait(dve, u_done, 2 * i)
                split(g_s, g[:, :, :], g_head, g_tail, i)

            def gate_tails(i):
                dve.wait_ge(gg_head, i + 1)
                nc.vector.tensor_tensor(gg_s[:, 1], gg[:, :, :], gg_s[:, 0], ALU.subtract).then_inc(gg_tail, 1)

            def deltas(i):
                dve.wait_ge(lz_r, i + 1)
                dve.wait_ge(rz_r, i + 1)
                wait(dve, dq_r, 2 * i)
                wait(dve, decay_r, i)
                nc.vector.tensor_tensor(delta[:, :], rz[:, :], az[:, :], ALU.add).then_inc(delta_r, 1)

            def gelu_tails(j):
                for k in range(HC):
                    dve.wait_ge(h_head, HC * j + k + 1)
                    nc.vector.tensor_tensor(h_s[:, 1, k], hf[:, k % HR], h_s[:, 0, k], ALU.subtract)\
                        .then_inc(h_tail, 1)

            def scans(i):
                for c in range(KC):
                    dve.wait_ge(b_done, 2 * i + c + 1)
                    dve.wait_ge(u_r, 2 * i + c + 1)
                    nc.vector.scalar_tensor_tensor(q[:, c], bank[2 + c][:, :], state_b[:, c:c + 1], u[:, c],
                                                   ALU.add, ALU.mult).then_inc(q_r, 1)
                for c in range(KC):
                    dve.wait_ge(q_r, 2 * i + c + 1)
                    nc.vector.tensor_tensor(q[:, c], q[:, c], delta[:, :], ALU.mult).then_inc(dq_r, 1)
                for c in range(KC):
                    dve.wait_ge(dq_r, 2 * i + c + 1)
                    dve.wait_ge(decay_r, i + 1)
                    wait(dve, y_tail, i)
                    nc.vector.tensor_tensor_scan(y[:, c], decay[:, :], q[:, c], 0.0, ALU.mult, ALU.add)\
                        .then_inc(y_r, 1)
                dve.wait_ge(y_head, i + 1)
                nc.vector.tensor_tensor(y_s[:, 1], y[:, :, :], y_s[:, 0], ALU.subtract).then_inc(y_tail, 1)

            def norm3(j):
                dve.wait_ge(xres_r, j + 1)
                for h in range(2):
                    dve.wait_ge(o_done, 2 * j + h + 1)
                    wait(dve, xp_r, 4 * j)
                    nc.vector.tensor_tensor(v[:, 2 * h:2 * h + 2], token_pair(6 + h), x_res[:, 2 * h:2 * h + 2],
                                            ALU.add).then_inc(v_r, 1)
                dve.wait_ge(v_r, 2 * j + 2)
                stats(v, st3, st3_r, mv3, mv3_r, j, None)

            def norm3_rows(j):
                wait(dve, xp_stored, 16 * j)
                normalise(xp, v, mv3, rs3, rs3_r, xp_r, j)

            def first():
                norm1(0, 0)
                norm1_split(0)

            def step(i, par):
                if not is_first(i):
                    norm2_split(i - 1)
                gates(i)
                gate_tails(i)
                if not is_first(i):
                    gelu_tails(i - 1)
                deltas(i)
                if not is_last(i):
                    norm1(i + 1, 1 - par)
                scans(i)
                if not is_last(i):
                    norm1_split(i + 1)
                if not is_first(i):
                    norm3(i - 1)
                norm2(i)
                if not is_first(i):
                    norm3_rows(i - 1)
                norm2_rows(i)

            def last():
                norm2_split(LAST)
                gelu_tails(LAST)
                norm3(LAST)
                norm3_rows(LAST)

            over_batches(dve, first, step, last)

        @block.tensor
        def _(pe):
            pe.wait_ge(ident_done, 3)

            def turn(src, banks, done):
                for c in range(KC):
                    for n in range(TT):
                        last = nc.tensor.transpose(bank[banks[c]][:, n * P:(n + 1) * P],
                                                   src[:, n, c * P:(c + 1) * P], ident[:, :])
                    last.then_inc(done, 1)

            def turn1(i):
                pe.wait_ge(z1_r, TT * i + TT)
                wait(pe, u_r, 2 * i)
                turn(z1, (0, 1), zT_done)

            def gates(i):
                pe.wait_ge(xn_tail, i + 1)
                for c in range(2 * KC):
                    if c >= KC:
                        wait(pe, x1_r, 2 * (i - 1) + c - KC + 1)
                    split_product(nc, bank[c][:, :], lambda s, k: gate_w[:, s, k, c * P:(c + 1) * P],
                                  lambda s, k: xn_s[:, s, k], KC).then_inc(gate_done, 1)

            def step_size(i):
                wait(pe, az_r, i)
                wait(pe, rz_r, i)
                split_product(nc, bank[4][:, :], lambda s, k: mean_w[:, s, k], lambda s, k: xn_s[:, s, k], KC)\
                    .then_inc(zz_done, 1)

            def turn2(j):
                pe.wait_ge(z2_r, TT * j + TT)
                wait(pe, hf_r, HC * j)
                wait(pe, v_r, 2 * j)
                turn(z2, (5, 6), z2T_done)

            def mlp_up(j):
                pe.wait_ge(xn2_tail, j + 1)
                for m in range(HC):
                    if m >= 3:
                        pe.wait_ge(hf_r, HC * j + m - 2)
                    split_product(nc, bank[5 + (2 + m) % 3][:, :], lambda s, k: mlp_w1[:, s, k, m * P:(m + 1) * P],
                                  lambda s, k: xn2_s[:, s, k], KC).then_inc(m_done, 1)

            def states(i):
                pe.wait_ge(g_tail, i + 1)
                pe.wait_ge(g_r, 4 * i + 4)
                for c in range(KC):
                    split_product(nc, bank[c][:, :], lambda s, k: state_w[:, s, k, c * P:(c + 1) * P],
                                  lambda s, k: g_s[:, s, k], KC).then_inc(u_done, 1)
                pe.wait_ge(gg_tail, i + 1)
                for c in range(KC):
                    split_product(nc, bank[2 + c][:, :], lambda s, k: state_w[:, s, k, c * P:(c + 1) * P],
                                  lambda s, k: gg_s[:, s, k], KC).then_inc(b_done, 1)

            def mlp_down(j, halves):
                pe.wait_ge(h_tail, HC * j + HC)
                for h in halves:
                    for n in (2 * h, 2 * h + 1):
                        last = split_product(nc, token_pair(6 + h)[:, n % 2], lambda s, k: h_s[:, s, k, n * P:(n + 1) * P],
                                             lambda s, k: mlp_w2[:, s, k], HC)
                    last.then_inc(o_done, 1)

            def project(i):
                pe.wait_ge(y_tail, i + 1)
                for h in range(2):
                    pe.wait_ge(q_r, 2 * i + h + 1)
                    for n in (2 * h, 2 * h + 1):
                        last = split_product(nc, token_pair(2 + h)[:, n % 2], lambda s, k: y_s[:, s, k, n * P:(n + 1) * P],
                                             lambda s, k: out_w[:, s, k], KC)
                    last.then_inc(out_done, 1)

            def step(i, par):
                if is_first(i):
                    pe.wait_ge(w_tail, len(weights))
                    pe.wait_ge(mean_done, 6)
                gates(i)
                if not is_first(i):
                    turn2(i - 1)
                step_size(i)
                if not is_first(i):
                    mlp_up(i - 1)
                states(i)
                if not is_first(i):
                    mlp_down(i - 1, (0,))
                if not is_last(i):
                    turn1(i + 1)
                if not is_first(i):
                    mlp_down(i - 1, (1,))
                project(i)

            def last():
                turn2(LAST)
                mlp_up(LAST)
                mlp_down(LAST, (0, 1))

            over_batches(pe, lambda: turn1(0), step, last)

    numbers = sorted(s.num for s in used)
    nc.gpsimd.sem_clear(range(numbers[0], numbers[-1] + 1))
    nc.all_engine_barrier()


GENS = 3
XR = 4
SQ_MAX = 20

R177 = 177.0 ** 0.5
C3 = 2.0 / 3.0
C1, C2 = C3 * (1 + R177) / 88, C3 * (1 + R177) / 352
C4 = (-271 + 29 * R177) / (315 * C3)
C5, C6 = 11 * (-1 + R177) / (1260 * C3), 11 * (-9 + R177) / (5040 * C3)
C7 = (89 - R177) / (5040 * C3 * C3)
CY2 = (857 - 58 * R177) / 630



def moe_half(nc, t, xp_dram, ab_dram, abx_dram, zs_dram, ys_dram, out):
    keep = ExitStack()
    with keep:
        def ksb(name, shape, dt=F32):
            return keep.enter_context(nc.sbuf_tensor(name, shape, dt))

        ident = ksb("ident_b", [P, P])
        w1_s = ksb("w1_s", [P, 2, NE * KC * FE], BF16)
        w2_s = ksb("w2_s", [P, 2, NE * FC * D], BF16)
        eb1 = ksb("eb1", [P, NE * FC])
        eb2r = ksb("eb2r", [NE, D])
        eb2 = ksb("eb2", [NE, D])
        gamma, beta = ksb("gamma", [P, KC]), ksb("beta", [P, KC])
        gc1_row, gc2_row, gc_b = ksb("gc1_row", [P, D]), ksb("gc2_row", [P, D]), ksb("gc_b", [P, 1])
        neg_half = ksb("neg_half_b", [P, TT])
        eps_t = ksb("eps_t_b", [P, TT])
        wdense = ksb("wdense", [P, NTILES, NE])
        wtop = ksb("wtop", [P, 2, NTILES])
        gate_part = ksb("gate_part", [P, NTILES])
        tile_expert = ksb("tile_expert", [P, QT], I32)
        plan(nc, t, locals(), xp_dram, ab_dram, abx_dram, zs_dram)
        experts(nc, locals(), zs_dram, ys_dram)
        combine(nc, locals(), ab_dram, abx_dram, ys_dram, out)


def plan(nc, t, kept, xp_dram, ab_dram, abx_dram, zs_dram):
    (ident, w1_s, w2_s, eb1, eb2r, eb2, gamma, beta, gc1_row, gc2_row, gc_b, neg_half, eps_t, wdense, wtop,
     gate_part, tile_expert) = [kept[n] for n in (
        "ident", "w1_s", "w2_s", "eb1", "eb2r", "eb2", "gamma", "beta", "gc1_row", "gc2_row", "gc_b",
        "neg_half", "eps_t", "wdense", "wtop", "gate_part", "tile_expert")]
    ctx = ExitStack()
    with ctx:
        def sb(name, shape, dt=F32):
            return ctx.enter_context(nc.sbuf_tensor(name, shape, dt))

        def pb(name, shape, dt=F32):
            return ctx.enter_context(nc.psum_tensor(name, shape, dt))

        def sem(name):
            return ctx.enter_context(nc.semaphore(name))

        bank = [pb(f"pbank{k}", [P, 512]) for k in range(8)]
        tri, ones = sb("tri", [P, P], BF16), sb("ones", [P, P], BF16)
        ones32 = sb("ones32", [P, NTILES])
        iota8i, iota8 = sb("iota8i", [P, NE], I32), sb("iota8", [P, NE])
        iota16i, iota16 = sb("iota16i", [P, 16], I32), sb("iota16", [P, 16])
        iotaqi, iotaq = sb("iotaqi", [P, QT], I32), sb("iotaq", [P, QT])
        thr = sb("thr", [P, SQ_MAX - 1])
        A, A2, U, L, X = [sb(n, [P, GENS, KC, D]) for n in ("gA", "gA2", "gU", "gL", "gX")]
        aT_s, b_s = [sb(n, [P, GENS, 2, KC, D], BF16) for n in ("aT_s", "b_s")]
        rows_sum, norm, hits = sb("rows_sum", [P, GENS * KC]), sb("norm", [P, 2]), sb("hits", [P, SQ_MAX - 1])
        sq_f, sq_i = sb("sq_f", [P, 3]), sb("sq_i", [P, 2], I32)
        w1_f = sb("w1_f", [P, 2, KC * FE])
        w2t_01 = sb("w2t_f", [P, 2, KC * FE])
        w2_01 = sb("w2_f", [P, 2, FC * D])
        w2t_s = sb("w2t_s", [P, 2, 2, KC * FE], BF16)
        pos = sb("pos", [P, 2, NTILES], U32)
        home = sb("home", [P, 2, NTILES], I32)
        eb2t = sb("eb2t", [P, KC, NE])
        abel_f, abel_s, abel_b = sb("abel_f", [P, KC, D]), sb("abel_s", [P, 2, KC, D], BF16), sb("abel_b", [P, D])
        mgw, mgb = sb("mgw", [P, KC, NE]), sb("mgb", [P, NE])
        xp = sb("xp_b", [P, XR, TT, D])
        slot_of_xp = [xp[:, k].rearrange("p t d -> p (t d)") for k in range(XR)]
        w2t_f = [w2t_01[:, 0], w2t_01[:, 1], slot_of_xp[1], slot_of_xp[2]]
        w2_f = [w2_01[:, 0], w2_01[:, 1], slot_of_xp[3], slot_of_xp[0]]
        st, mv, rs = sb("st_b", [P, TT, 6]), sb("mv_b", [P, TT, 2]), sb("rs_b", [P, TT])
        z3 = sb("z3", [P, NTILES, ROW])
        xn3 = A2[:, 0:2].rearrange("p g c d -> p g (c d)")
        xn3_s = U[:, 0:2].bitcast(BF16)
        abel = [m[:, 0:2].rearrange("p g c d -> p (g c) d") for m in (A, L)]
        abx = X[:, 0:2].rearrange("p g c d -> p (g c) d")
        scrap = b_s[:, 0].rearrange("p s k d -> p (s k) d")
        logits = sb("logits", [P, NTILES, NE])
        top = sb("top", [P, NTILES, 8])
        topi = sb("topi", [P, NTILES, 8], U32)
        topf = sb("topf", [P, 2, NTILES])
        oh = sb("oh", [P, 2, NTILES, NE])
        picked = sb("picked", [P, NTILES, NE], BF16)
        tot, cum, slot, prod = [xp[:, 0, n].rearrange("p (n e) -> p n e", e=NE) for n in range(4)]
        ntile, cumt, base = sb("ntile", [P, NE]), sb("cumt", [P, NE]), sb("base", [P, NE])
        over, below = sb("over", [P, NE, 16]), sb("below", [P, QT, NE])
        tef, posf = sb("tef", [P, QT]), sb("posf", [P, NTILES])
        td = sb("td", [P, NTILES])

        vec_in, gens_in, const_done = [sem(n) for n in ("p_vec_in", "p_gens_in", "p_const")]
        norm_r, all_norm, sq_r, step = [sem(n) for n in ("p_norm_r", "p_all_norm", "p_sq_r", "p_step")]
        mat_r, b_head, turned, a_head, split_r, prod_done = [sem(n) for n in (
            "p_mat_r", "p_b_head", "p_turned", "p_a_head", "p_split_r", "p_prod_done")]
        w_in = [sem(f"p_w_in{k}") for k in range(4)]
        w_head, w_tail, fold_done, w2_r, w2_head, w2_tail = [sem(n) for n in (
            "p_w_head", "p_w_tail", "p_fold_done", "p_w2_r", "p_w2_head", "p_w2_tail")]
        eb_done, eb_r = sem("p_eb_done"), sem("p_eb_r")
        xp_in = [sem(f"p_xp_in{k}") for k in range(XR)]
        st_r, mv_r, ve_r, rs_r, z3_r = [sem(n) for n in (
            "p_st_r", "p_mv_r", "p_ve_r", "p_rs_r", "p_z3_r")]
        zT_done, xn_r, xn_head, xn_tail, lg_done, lg_r, ab_done, ab_r, gelu_r, top_r = [sem(n) for n in (
            "p_zT_done", "p_xn_r", "p_xn_head", "p_xn_tail", "p_lg_done", "p_lg_r", "p_ab_done", "p_ab_r",
            "p_gelu_r", "p_top_r")]
        ab_stored = [sem("p_ab_stored0"), sem("p_ab_stored1")]
        w1_in = [sem("p_w1_in0"), sem("p_w1_in1")]
        w1_head, w1_tail, part_r, abx_r, abx_stored, home_r, home_set = [sem(n) for n in (
            "p_w1_head", "p_w1_tail", "p_part_r", "p_abx_r", "p_abx_stored", "p_home_r", "p_home_set")]
        gap_r, gap_exp, picked_r, rank_done, pos_r, sent = [sem(n) for n in (
            "p_gap_r", "p_gap_exp", "p_picked_r", "p_rank_done", "p_pos_r", "p_sent")]

        vectors = [(ident, "ident"), (eb1, "eb1"), (eb2, "eb2"), (gamma, "gamma"), (beta, "beta"),
                   (gc1_row, "gc1_row"), (gc2_row, "gc2_row"), (gc_b, "gc_b"), (abel_b, "abel_b"), (mgb, "mgb")]
        vectors = [(a, n) for a, n in vectors if n != "ident"]
        NV = 16 * (len(vectors) + 3)

        def pair(k):
            return bank[k][:, :].rearrange("p (t d) -> p t d", t=2)

        def mat(k):
            return bank[k][:, :].rearrange("p (c d) -> p c d", c=KC)

        def of_tile(x, b):
            return x[:, bass.ds(b * TT, TT)]

        block = ctx.enter_context(nc.Block())

        @block.sync
        def _(sp):
            def load_xp(b):
                wait(sp, abx_r, b - XR + 1)
                sp.dma_start(xp[:, b % XR], xp_dram[b].rearrange("(t p) d -> p t d", p=P)).then_inc(xp_in[b % XR], 16)

            def load_w1(e, par):
                wait(sp, w1_tail, e - 1)
                sp.dma_start(w1_f[:, par].rearrange("p (k n) -> p k n", k=KC),
                             t["ew1"][bass.ds(e, 1)].rearrange("e (k p) n -> p (e k) n", p=P)).then_inc(w1_in[par], 16)

            def load_expert(e):
                wait(sp, w2_tail, e - 3)
                sp.dma_start(w2t_f[e % 4].rearrange("p (k n) -> p k n", k=KC),
                             t["ew2t"][e].rearrange("(k p) n -> p k n", p=P)).then_inc(w_in[e % 4], 16)
                sp.dma_start(w2_f[e % 4].rearrange("p (k n) -> p k n", k=FC),
                             t["ew2"][e].rearrange("(k p) n -> p k n", p=P)).then_inc(w_in[e % 4], 16)

            def store_abel(b, par):
                sp.wait_ge(gelu_r, TT // 2 * (b + 1))
                sp.dma_start(ab_dram[bass.ds(b, 1)].rearrange("b (t p) d -> p (b t) d", p=P), abel[par])\
                    .then_inc(ab_stored[par], 16)

            def store_abx(b):
                sp.wait_ge(abx_r, b + 1)
                sp.dma_start(abx_dram[bass.ds(b, 1)].rearrange("b (t p) d -> p (b t) d", p=P), abx)\
                    .then_inc(abx_stored, 16)

            load_xp(0)
            for tile, name in vectors:
                sp.dma_start(tile[:, :], t[name]).then_inc(vec_in, 16)
            sp.dma_start(eb2t[:, :, :], t["eb2t"].rearrange("(k p) n -> p k n", p=P)).then_inc(vec_in, 16)
            sp.dma_start(mgw[:, :, :], t["mgw"].rearrange("(k p) n -> p k n", p=P)).then_inc(vec_in, 16)
            sp.dma_start(abel_f[:, :, :], t["abel_w"].rearrange("(k p) n -> p k n", p=P)).then_inc(vec_in, 16)
            for b in range(1, XR):
                load_xp(b)
            load_w1(0, 0)
            load_w1(1, 1)
            load_expert(0)
            load_expert(1)
            for b in range(BATCHES):
                if b + XR < BATCHES:
                    load_xp(b + XR)
                if b + 2 < NE:
                    load_w1(b + 2, b % 2)
                store_abel(b, b % 2)
                store_abx(b)
            for s in ab_stored:
                sp.wait_ge(s, 16 * BATCHES // 2)
            sp.wait_ge(abx_stored, 16 * BATCHES)
            sp.dma_start(A[:, :, :, :], t["gens"].rearrange("g (k p) n -> p g k n", p=P)).then_inc(gens_in, 16)
            sp.wait_ge(pos_r, 2)
            for e in range(2, NE):
                load_expert(e)

        @block.gpsimd
        def _(pool):
            nc.gpsimd.memset(neg_half[:, :], -0.5).then_inc(const_done, 1)
            nc.gpsimd.memset(ident[:, :], 0.0)
            nc.gpsimd.memset(eps_t[:, :], EPS)
            nc.gpsimd.memset(tri[:, :], 1.0)
            nc.gpsimd.memset(ones[:, :], 1.0)
            nc.gpsimd.memset(ones32[:, :], 1.0)
            for k in range(SQ_MAX - 1):
                nc.gpsimd.memset(thr[:, k:k + 1], float(2 ** k))
            nc.gpsimd.iota(iota8i[:, :], [[1, NE]], base=0, channel_multiplier=0)
            nc.gpsimd.iota(iota16i[:, :], [[1, 16]], base=0, channel_multiplier=0)
            nc.gpsimd.iota(iotaqi[:, :], [[1, QT]], base=0, channel_multiplier=0).then_inc(const_done, 1)
            pool.wait_ge(const_done, 2)
            nc.gpsimd.affine_select(out=ident[:, :], in_=ident[:, :], compare_op=ALU.not_equal, fill=1.0,
                                    base=0, pattern=[[-1, P]], channel_multiplier=1)
            nc.gpsimd.affine_select(out=tri[:, :], in_=tri[:, :], compare_op=ALU.is_gt, fill=0.0,
                                    base=0, pattern=[[1, P]], channel_multiplier=-1).then_inc(const_done, 1)
            for r in range(2):
                nc.gpsimd.iota(home[:, r], [[P, NTILES]], base=r * NTILES * P, channel_multiplier=1)\
                    .then_inc(home_r, 1)

            def rstd(b):
                pool.wait_ge(mv_r, TT * b + TT)
                nc.gpsimd.tensor_tensor(rs[:, :], mv[:, :, 1], eps_t[:, :], ALU.add).then_inc(ve_r, 1)
                pool.wait_ge(ve_r, b + 1)
                nc.gpsimd.tensor_tensor(rs[:, :], rs[:, :], neg_half[:, :], ALU.pow).then_inc(rs_r, 1)

            with pool.Fori(0, BATCHES) as b:
                rstd(b)
            pool.wait_ge(norm_r, 2)
            nc.gpsimd.partition_all_reduce(norm[:, 1:2], norm[:, 0:1], P, bass.bass_isa.ReduceOp.max)\
                .then_inc(all_norm, 1)
            for r in range(2):
                pool.wait_ge(pos_r, r + 1)
                if r:
                    nc.gpsimd.tensor_copy(z3[:, :, D].bitcast(I32), home[:, 1]).then_inc(home_set, 1)
                pool.wait_ge(home_set, r + 1)
                for n in range(NTILES):
                    nc.gpsimd.indirect_dma_start(
                        out=zs_dram[:, :], out_offset=bass.IndirectOffsetOnAxis(ap=pos[:, r, n:n + 1], axis=0),
                        in_=z3[:, n, :], in_offset=None).then_inc(sent, 16)
                pool.wait_ge(sent, 16 * NTILES * (r + 1))

        @block.scalar
        def _(act):
            def norm(b):
                for c in range(KC):
                    act.wait_ge(zT_done, 2 * b + c + 1)
                    wait(act, xn_tail, b)
                    wait(act, lg_done, b)
                    nc.scalar.activation(xn3[:, c], bank[c][:, :], ACT.Identity, bias=beta[:, c:c + 1],
                                         scale=gamma[:, c:c + 1]).then_inc(xn_r, 1)

            def w1_heads(e, par):
                act.wait_ge(w1_in[par], (e - par) * 8 + 16)
                nc.scalar.activation(w1_s[:, 0, bass.ds(e * (KC * FE), KC * FE)], w1_f[:, par], ACT.Copy)\
                    .then_inc(w1_head, 1)

            def gelus(b, par):
                for h in range(2):
                    act.wait_ge(ab_r, 2 * b + h + 1)
                    nc.scalar.activation(abel[par][:, 2 * h:2 * h + 2], abel[par][:, 2 * h:2 * h + 2], ACT.Gelu)\
                        .then_inc(gelu_r, 1)

            act.wait_ge(vec_in, NV)
            nc.scalar.activation(abel_s[:, 0], abel_f[:, :, :], ACT.Copy).then_inc(w_head, 1)
            norm(0)
            w1_heads(0, 0)
            for b in range(BATCHES):
                if b + 1 < BATCHES:
                    norm(b + 1)
                gelus(b, b % 2)
                if b + 1 < BATCHES:
                    w1_heads(b + 1, (b + 1) % 2)
            act.wait_ge(gap_r, 1)
            nc.scalar.activation(td[:, :], td[:, :], ACT.Exp).then_inc(gap_exp, 1)

            def heads(n, slot, need, a_slot):
                act.wait_ge(mat_r, need)
                nc.scalar.activation(b_s[:, slot, 0], b_of(n, slot), ACT.Copy).then_inc(b_head, 1)
                act.wait_ge(turned, n + 1)
                nc.scalar.activation(aT_s[:, slot, 0], mat(slot), ACT.Copy).then_inc(a_head, 1)

            def b_of(n, slot):
                if isinstance(n, int):
                    return (A, U, U)[n // GENS][:, slot]
                return X[:, slot]

            for n in range(3 * GENS):
                heads(n, n % GENS, n + 1, None)
            act.wait_ge(sq_r, 4)
            squarings = act.value_load(sq_i[0:1, 0:1], min_val=1, max_val=SQ_MAX)
            with act.Fori(0, squarings) as k:
                for s in range(GENS):
                    heads(k * GENS + (3 * GENS + s), s, k * GENS + (3 * GENS + s + 1), None)
            after = squarings * GENS + 3 * GENS
            heads(after, 1, after + 3, 0)
            heads(after + 1, 2, after + 4, 1)
            act.wait_ge(mat_r, after + 5)
            nc.scalar.activation(b_s[:, 0, 0], L[:, 0], ACT.Copy).then_inc(b_head, 1)

            def expert_heads(e):
                act.wait_ge(w_in[e % 4], e // 4 * 32 + 32)
                wait(act, fold_done, 2 * (e - 1))
                nc.scalar.activation(w2t_s[:, e % 2, 0], w2t_f[e % 4], ACT.Copy).then_inc(w_head, 1)

            expert_heads(0)
            for e in range(NE):
                if e + 1 < NE:
                    expert_heads(e + 1)
                act.wait_ge(w2_r, 2 * e + 2)
                nc.scalar.activation(w2_s[:, 0, e * (FC * D):(e + 1) * (FC * D)], w2_f[e % 4], ACT.Copy)\
                    .then_inc(w2_head, 1)

        @block.vector
        def _(dve):
            links = [0]

            def link(*ins):
                for i in ins:
                    i.then_inc(step, 1)
                links[0] += len(ins)
                dve.wait_ge(step, links[0])

            def stats(b):
                dve.wait_ge(xp_in[b % XR], 16 * (b // XR + 1))
                for n in range(TT):
                    nc.vector.bn_stats(st[:, n], xp[:, b % XR, n]).then_inc(st_r, 1)
                for n in range(TT):
                    dve.wait_ge(st_r, TT * b + n + 1)
                    nc.vector.bn_aggr(mv[:, n], st[:, n]).then_inc(mv_r, 1)

            def normalise(b):
                dve.wait_ge(rs_r, b + 1)
                for n in range(TT):
                    nc.vector.tensor_scalar(z3[:, b * TT + n, 0:D], xp[:, b % XR, n], mv[:, n, 0:1], rs[:, n:n + 1],
                                            ALU.subtract, ALU.mult).then_inc(z3_r, 1)

            def split(b):
                dve.wait_ge(xn_r, 2 * b + 2)
                wait(dve, ab_done, 2 * b)
                nc.vector.tensor_copy(xn3_s[:, 0], xn3[:, :, :]).then_inc(xn_head, 1)
                dve.wait_ge(xn_head, b + 1)
                nc.vector.tensor_tensor(xn3_s[:, 1], xn3[:, :, :], xn3_s[:, 0], ALU.subtract).then_inc(xn_tail, 1)

            def w1_tails(e, par):
                dve.wait_ge(w1_head, e + 1)
                nc.vector.tensor_tensor(w1_s[:, 1, bass.ds(e * (KC * FE), KC * FE)], w1_f[:, par],
                                        w1_s[:, 0, bass.ds(e * (KC * FE), KC * FE)], ALU.subtract).then_inc(w1_tail, 1)

            def projected(b, par):
                dve.wait_ge(lg_done, b + 1)
                nc.vector.tensor_tensor(of_tile(logits, b),
                                        bank[2][:, 0:TT * NE].rearrange("p (t e) -> p t e", t=TT),
                                        mgb[:, :].rearrange("p (a e) -> p a e", a=1).to_broadcast([P, TT, NE]),
                                        ALU.add).then_inc(lg_r, 1)
                for h in range(2):
                    dve.wait_ge(ab_done, 2 * b + h + 1)
                    if not (isinstance(b, int) and b < 2):
                        dve.wait_ge(ab_stored[par], (b - par) * 8)
                    nc.vector.tensor_tensor(abel[par][:, 2 * h:2 * h + 2], pair(3 + h),
                                            abel_b[:, :].rearrange("p (a d) -> p a d", a=1).to_broadcast([P, 2, D]),
                                            ALU.add).then_inc(ab_r, 1)

            def branch(b, par):
                dve.wait_ge(gelu_r, 2 * b + 2)
                wait(dve, part_r, TT * b)
                for n in range(TT):
                    nc.vector.scalar_tensor_tensor(scrap[:, n], abel[par][:, n], 1.0, gc1_row[:, :], ALU.mult, ALU.mult,
                                                   accum_out=gate_part[:, bass.ds(b * TT + n, 1)])\
                        .then_inc(part_r, 1)
                wait(dve, abx_stored, 16 * b)
                nc.vector.scalar_tensor_tensor(abx, xp[:, b % XR], 2.0, abel[par], ALU.mult, ALU.add).then_inc(abx_r, 1)

            stats(0)
            normalise(0)
            stats(1)
            dve.wait_ge(vec_in, NV)
            dve.wait_ge(w_head, 1)
            nc.vector.tensor_tensor(abel_s[:, 1], abel_f[:, :, :], abel_s[:, 0], ALU.subtract).then_inc(w_tail, 1)
            for b in range(BATCHES):
                if b + 1 < BATCHES:
                    normalise(b + 1)
                split(b)
                w1_tails(b, b % 2)
                if b >= 1:
                    branch(b - 1, 1 - b % 2)
                if b + 2 < BATCHES:
                    stats(b + 2)
                projected(b, b % 2)
            branch(BATCHES - 1, (BATCHES - 1) % 2)
            dve.wait_ge(home_r, 2)
            link(nc.vector.tensor_copy(z3[:, :, D].bitcast(I32), home[:, 0]))
            dve.sem_inc(home_set, 1)

            dve.wait_ge(lg_r, BATCHES)
            for n in range(NTILES):
                nc.vector.max(top[:, n], logits[:, n]).then_inc(top_r, 1)
            for n in range(NTILES):
                dve.wait_ge(top_r, n + 1)
                ins = nc.vector.max_index(topi[:, n], top[:, n], logits[:, n])
            link(ins)
            i0 = nc.vector.tensor_copy(topf[:, :, :].rearrange("p r n -> p n r"), topi[:, :, 0:2])
            nc.vector.tensor_tensor(td[:, :], top[:, :, 1], top[:, :, 0], ALU.subtract).then_inc(gap_r, 1)
            link(i0, nc.vector.tensor_copy(iota8[:, :], iota8i[:, :]),
                 nc.vector.tensor_copy(iota16[:, :], iota16i[:, :]),
                 nc.vector.tensor_copy(iotaq[:, :], iotaqi[:, :]))

            def over_e(x):
                return x.rearrange("p (n a) -> p n a", a=1).to_broadcast([P, NTILES, NE])

            def over_n(x):
                return x.rearrange("p (a e) -> p a e", a=1).to_broadcast([P, NTILES, NE])

            link(*[nc.vector.tensor_tensor(oh[:, r], over_n(iota8[:, :]), over_e(topf[:, r]), ALU.is_equal)
                   for r in range(2)],
                 nc.vector.tensor_scalar(iota16[:, :], iota16[:, :], float(SLOT), None, ALU.mult))
            nc.vector.tensor_tensor(picked[:, :, :], oh[:, 0], oh[:, 1], ALU.add).then_inc(picked_r, 1)
            dve.wait_ge(gap_exp, 1)
            link(nc.vector.tensor_scalar(wtop[:, 0], td[:, :], 1.0, None, ALU.add))
            link(nc.vector.reciprocal(wtop[:, 0], wtop[:, 0]))
            link(nc.vector.tensor_tensor(wtop[:, 1], td[:, :], wtop[:, 0], ALU.mult))
            link(nc.vector.tensor_tensor(wdense[:, :, :], oh[:, 0], over_e(wtop[:, 0]), ALU.mult),
                 nc.vector.tensor_tensor(prod[:, :, :], oh[:, 1], over_e(wtop[:, 1]), ALU.mult))
            dve.wait_ge(rank_done, 2)
            link(nc.vector.tensor_tensor(wdense[:, :, :], wdense[:, :, :], prod[:, :, :], ALU.add),
                 nc.vector.tensor_copy(tot[:, :, :], bank[6][:, 0:NTILES * NE].rearrange("p (n e) -> p n e", e=NE)))
            link(*[nc.vector.tensor_tensor_scan(cum[:, :, e], ones32[:, :], tot[:, :, e], 0.0, ALU.mult, ALU.add)
                   for e in range(NE)])
            link(nc.vector.tensor_tensor(slot[:, :, :], cum[:, :, :], tot[:, :, :], ALU.subtract),
                 nc.vector.tensor_tensor(
                     over[:, :, :],
                     cum[:, NTILES - 1, :].rearrange("p (e a) -> p e a", a=1).to_broadcast([P, NE, 16]),
                     iota16[:, :].rearrange("p (a m) -> p a m", a=1).to_broadcast([P, NE, 16]), ALU.is_gt))
            link(nc.vector.tensor_tensor(slot[:, :, :], slot[:, :, :],
                                         bank[5][:, 0:NTILES * NE].rearrange("p (n e) -> p n e", e=NE), ALU.add),
                 nc.vector.reduce_sum(ntile[:, :], over[:, :, :], AX.X))
            link(nc.vector.tensor_tensor_scan(cumt[:, :], ones32[:, 0:NE], ntile[:, :], 0.0, ALU.mult, ALU.add))
            link(nc.vector.tensor_tensor(base[:, :], cumt[:, :], ntile[:, :], ALU.subtract),
                 nc.vector.tensor_tensor(
                     below[:, :, :],
                     cumt[:, :].rearrange("p (a e) -> p a e", a=1).to_broadcast([P, QT, NE]),
                     iotaq[:, :].rearrange("p (q a) -> p q a", a=1).to_broadcast([P, QT, NE]), ALU.is_le))
            link(nc.vector.tensor_scalar(base[:, :], base[:, :], float(SLOT), None, ALU.mult),
                 nc.vector.reduce_sum(tef[:, :], below[:, :, :], AX.X))
            link(nc.vector.tensor_tensor(slot[:, :, :], slot[:, :, :], over_n(base[:, :]), ALU.add),
                 nc.vector.tensor_scalar(tef[:, :], tef[:, :], float(NE - 1), None, ALU.min))
            link(nc.vector.tensor_copy(tile_expert[:, :], tef[:, :]))
            for r in range(2):
                link(nc.vector.tensor_tensor(prod[:, :, :], slot[:, :, :], oh[:, r], ALU.mult))
                link(nc.vector.reduce_sum(posf[:, :], prod[:, :, :], AX.X))
                nc.vector.tensor_copy(pos[:, r], posf[:, :]).then_inc(pos_r, 1)
                dve.wait_ge(pos_r, r + 1)

            dve.wait_ge(gens_in, 16)
            nc.vector.tensor_reduce(rows_sum[:, :], A[:, :, :, :].rearrange("p g k n -> p (g k) n"), AX.X, ALU.add,
                                    apply_absolute_value=True).then_inc(norm_r, 1)
            dve.wait_ge(norm_r, 1)
            nc.vector.reduce_max(norm[:, 0:1], rows_sum[:, :], AX.X).then_inc(norm_r, 1)
            dve.wait_ge(const_done, 3)
            dve.wait_ge(all_norm, 1)
            link(nc.vector.tensor_scalar(hits[:, :], thr[:, :], norm[:, 1:2], None, ALU.is_lt))
            nc.vector.reduce_sum(sq_f[:, 0:1], hits[:, :], AX.X).then_inc(sq_r, 1)
            dve.wait_ge(sq_r, 1)
            nc.vector.tensor_scalar(sq_f[:, 1:2], sq_f[:, 0:1], 1.0, None, ALU.add).then_inc(sq_r, 1)
            dve.wait_ge(sq_r, 2)
            nc.vector.tensor_scalar(sq_f[:, 2:3], sq_f[:, 1:2], -float(2 ** 23), float(127 * 2 ** 23),
                                    ALU.mult, ALU.add).then_inc(sq_r, 1)
            dve.wait_ge(sq_r, 3)
            nc.vector.tensor_copy(sq_i[:, :], sq_f[:, 1:3]).then_inc(sq_r, 1)
            dve.wait_ge(sq_r, 4)
            for s in range(GENS):
                nc.vector.tensor_scalar(A[:, s], A[:, s], sq_i[:, 1:2].bitcast(F32), None, ALU.mult)\
                    .then_inc(mat_r, 1)

            def tails(n, slot, src, need):
                dve.wait_ge(mat_r, need)
                dve.wait_ge(b_head, n + 1)
                nc.vector.tensor_tensor(b_s[:, slot, 1], src, b_s[:, slot, 0], ALU.subtract).then_inc(split_r, 1)
                dve.wait_ge(a_head, n + 1)
                nc.vector.tensor_tensor(aT_s[:, slot, 1], mat(slot), aT_s[:, slot, 0], ALU.subtract)\
                    .then_inc(split_r, 1)

            def stt(dst, x, c, z):
                return nc.vector.scalar_tensor_tensor(dst, x, c, z, ALU.mult, ALU.add)

            for s in range(GENS):
                tails(s, s, A[:, s], s + 1)
            for s in range(GENS):
                dve.wait_ge(prod_done, s + 1)
                link(nc.vector.tensor_copy(A2[:, s], mat(3 + s)),
                     nc.vector.tensor_scalar(U[:, s], A[:, s], C1, None, ALU.mult))
                stt(U[:, s], A2[:, s], C2, U[:, s]).then_inc(mat_r, 1)
            for s in range(GENS):
                tails(GENS + s, s, U[:, s], GENS + s + 1)
            for s in range(GENS):
                dve.wait_ge(prod_done, GENS + s + 1)
                link(stt(L[:, s], A2[:, s], C3, mat(3 + s)),
                     nc.vector.tensor_scalar(U[:, s], A[:, s], C5, None, ALU.mult))
                link(stt(U[:, s], A2[:, s], C6 - C7 * C3, U[:, s]))
                stt(U[:, s], L[:, s], C7, U[:, s]).then_inc(mat_r, 1)
            for s in range(GENS):
                tails(2 * GENS + s, s, U[:, s], 2 * GENS + s + 1)
                link(stt(X[:, s], A2[:, s], CY2, A[:, s]))
                link(stt(X[:, s], L[:, s], C4, X[:, s]))
            for s in range(GENS):
                dve.wait_ge(prod_done, 2 * GENS + s + 1)
                nc.vector.tensor_tensor(X[:, s], X[:, s], mat(3 + s), ALU.add).then_inc(mat_r, 1)
            squarings = dve.value_load(sq_i[0:1, 0:1], min_val=1, max_val=SQ_MAX)
            with dve.Fori(0, squarings) as k:
                for s in range(GENS):
                    tails(k * GENS + (3 * GENS + s), s, X[:, s], k * GENS + (3 * GENS + s + 1))
                for s in range(GENS):
                    dve.wait_ge(prod_done, k * GENS + (3 * GENS + s + 1))
                    stt(X[:, s], X[:, s], 2.0, mat(3 + s)).then_inc(mat_r, 1)
            after = squarings * GENS + 3 * GENS
            dve.wait_ge(mat_r, after + 3)
            link(nc.vector.tensor_tensor(L[:, 0], X[:, 0], X[:, 1], ALU.add))
            tails(after, 1, X[:, 1], after + 3)
            dve.wait_ge(prod_done, after + 1)
            nc.vector.tensor_tensor(L[:, 0], L[:, 0], mat(3 + 1), ALU.add).then_inc(mat_r, 1)
            tails(after + 1, 2, X[:, 2], after + 4)
            dve.wait_ge(mat_r, after + 4)
            link(nc.vector.tensor_tensor(L[:, 1], L[:, 0], X[:, 2], ALU.add))
            dve.wait_ge(prod_done, after + 2)
            nc.vector.tensor_tensor(L[:, 0], L[:, 1], mat(3 + 2), ALU.add).then_inc(mat_r, 1)
            dve.wait_ge(b_head, after + 3)
            nc.vector.tensor_tensor(b_s[:, 0, 1], L[:, 0], b_s[:, 0, 0], ALU.subtract).then_inc(split_r, 1)
            dve.wait_ge(eb_done, 1)
            nc.vector.tensor_tensor(eb2r[:, :], eb2[:, :], bank[6][0:NE, 0:D], ALU.add).then_inc(eb_r, 1)

            def expert_tails(e):
                dve.wait_ge(w_head, e + 2)
                nc.vector.tensor_tensor(w2t_s[:, e % 2, 1], w2t_f[e % 4], w2t_s[:, e % 2, 0], ALU.subtract)\
                    .then_inc(w_tail, 1)

            def folded(e):
                for h in range(2):
                    dve.wait_ge(fold_done, 2 * e + h + 1)
                    part = w2_f[e % 4][:, h * 512:(h + 1) * 512]
                    nc.vector.tensor_tensor(part, part, bank[2 * (e % 2) + h][:, :], ALU.add).then_inc(w2_r, 1)
                dve.wait_ge(w2_head, e + 1)
                at = slice(e * (FC * D), (e + 1) * (FC * D))
                nc.vector.tensor_tensor(w2_s[:, 1, at], w2_f[e % 4], w2_s[:, 0, at], ALU.subtract).then_inc(w2_tail, 1)

            expert_tails(0)
            for e in range(NE):
                if e + 1 < NE:
                    expert_tails(e + 1)
                folded(e)

        @block.tensor
        def _(pe):
            pe.wait_ge(const_done, 3)

            def turn_tokens(b):
                pe.wait_ge(z3_r, TT * b + TT)
                wait(pe, xn_r, 2 * b)
                for c in range(KC):
                    for n in range(TT):
                        last = nc.tensor.transpose(bank[c][:, n * P:(n + 1) * P],
                                                   z3[:, b * TT + n, c * P:(c + 1) * P], ident[:, :])
                    last.then_inc(zT_done, 1)

            def route(b):
                pe.wait_ge(xn_r, 2 * b + 2)
                wait(pe, lg_r, b)
                for n in range(TT):
                    for k in range(KC):
                        last = nc.tensor.matmul(bank[2][:, n * NE:(n + 1) * NE], xn3[:, k, n * P:(n + 1) * P],
                                                mgw[:, k], start=k == 0, stop=k == KC - 1)
                last.then_inc(lg_done, 1)

            def project(b):
                pe.wait_ge(xn_tail, b + 1)
                wait(pe, ab_r, 2 * b)
                for n in range(TT):
                    last = split_product(nc, pair(3 + n // 2)[:, n % 2],
                                         lambda s, k: xn3_s[:, s, k, n * P:(n + 1) * P],
                                         lambda s, k: abel_s[:, s, k], KC)
                    if n % 2:
                        last.then_inc(ab_done, 1)

            turn_tokens(0)
            for b in range(BATCHES):
                route(b)
                if b + 1 < BATCHES:
                    turn_tokens(b + 1)
                project(b)
            pe.wait_ge(picked_r, 1)
            flat = picked[:, :, :].rearrange("p n e -> p (n e)")
            nc.tensor.matmul(bank[5][:, 0:NTILES * NE], tri[:, :], flat, start=True, stop=True).then_inc(rank_done, 1)
            nc.tensor.matmul(bank[6][:, 0:NTILES * NE], ones[:, :], flat, start=True, stop=True).then_inc(rank_done, 1)

            def turn(n, slot, src, need):
                pe.wait_ge(mat_r, need)
                for m in range(KC):
                    for k in range(KC):
                        last = nc.tensor.transpose(mat(slot)[:, k, m * P:(m + 1) * P],
                                                   src[:, m, k * P:(k + 1) * P], ident[:, :])
                last.then_inc(turned, 1)

            def product(n, slot):
                pe.wait_ge(split_r, n * 2 + 2)
                for m in range(KC):
                    last = split_product(nc, mat(3 + slot)[:, m], lambda s, k: aT_s[:, slot, s, k, m * P:(m + 1) * P],
                                         lambda s, k: b_s[:, slot, s, k], KC)
                last.then_inc(prod_done, 1)

            for r, src in enumerate((A, A2, L)):
                for s in range(GENS):
                    turn(r * GENS + s, s, src[:, s], r * GENS + s + 1)
                for s in range(GENS):
                    product(r * GENS + s, s)
            pe.wait_ge(sq_r, 4)
            squarings = pe.value_load(sq_i[0:1, 0:1], min_val=1, max_val=SQ_MAX)
            with pe.Fori(0, squarings) as k:
                for s in range(GENS):
                    turn(k * GENS + (3 * GENS + s), s, X[:, s], k * GENS + (3 * GENS + s + 1))
                for s in range(GENS):
                    product(k * GENS + (3 * GENS + s), s)
            after = squarings * GENS + 3 * GENS
            turn(after, 1, X[:, 0], after + 3)
            product(after, 1)
            turn(after + 1, 2, L[:, 0], after + 4)
            product(after + 1, 2)
            pe.wait_ge(split_r, after * 2 + 5)
            for k in range(KC):
                last = nc.tensor.matmul(bank[6][0:NE, 0:D], eb2t[:, k], L[:, 0, k], start=k == 0, stop=k == KC - 1)
            last.then_inc(eb_done, 1)

            def fold(e, par):
                pe.wait_ge(w_tail, e + 2)
                wait(pe, w2_r, 2 * (e - 1))
                for c in range(FC):
                    last = split_product(nc, pair(2 * par + c // 2)[:, c % 2],
                                         lambda s, k: w2t_s[:, par, s, k * FE + c * P:k * FE + (c + 1) * P],
                                         lambda s, k: b_s[:, 0, s, k], KC)
                    if c % 2:
                        last.then_inc(fold_done, 1)

            for e in (0, 1):
                fold(e, e)
            with pe.Fori(2, NE - 1, 2) as e:
                for par in range(2):
                    fold(e + par, par)


def experts(nc, kept, zs_dram, ys_dram):
    ident, w1_s, w2_s, eb1, gamma, beta, tile_expert = [kept[n] for n in (
        "ident", "w1_s", "w2_s", "eb1", "gamma", "beta", "tile_expert")]
    ctx = ExitStack()
    with ctx:
        def sb(name, shape, dt=F32):
            return ctx.enter_context(nc.sbuf_tensor(name, shape, dt))

        def pb(name, shape, dt=F32):
            return ctx.enter_context(nc.psum_tensor(name, shape, dt))

        def sem(name):
            return ctx.enter_context(nc.semaphore(name))

        zs = sb("zs", [P, 4, ST, ROW])
        place = sb("place", [P, 4, ST], U32)
        xe = sb("xe", [P, 2, KC, SLOT])
        xe_s = sb("xe_s", [P, 2, 2, KC, SLOT], BF16)
        hf = sb("hf_e", [P, 2, FC, SLOT])
        h_s = sb("h_s_e", [P, 2, 2, FC, SLOT], BF16)
        ye = sb("ye", [P, 2, ST, D])
        turn_bank = [pb(f"turn{i}", [P, KC, SLOT]) for i in range(2)]
        up_bank = [[pb(f"up{i}{j}", [P, 2, SLOT]) for j in range(2)] for i in range(2)]
        down_bank = [pb(f"down{i}", [P, ST, D]) for i in range(2)]
        zs_in = [sem(f"e_zs_in{k}") for k in range(4)]
        ys_out = [sem(f"e_ys_out{k}") for k in range(4)]
        ye_seen, placed = sem("e_ye_seen"), sem("e_placed")
        turned, xe_r, xe_head, xe_tail, up_done, hf_r, h_head, h_tail, down_done, ye_r = [sem(n) for n in (
            "e_turned", "e_xe_r", "e_xe_head", "e_xe_tail", "e_up_done", "e_hf_r", "e_h_head", "e_h_tail",
            "e_down_done", "e_ye_r")]
        block = ctx.enter_context(nc.Block())

        def over_tiles(eng, body, first=0, last=QT):
            for q in range(first, 4):
                body(q, q % 4)
            with eng.Fori(4, QT - 7, 4) as q:
                for k in range(4):
                    body(q + k, k)
            for q in range(QT - 4, last):
                body(q, q % 4)

        zs_v = zs_dram.rearrange("(q s p) d -> q p s d", s=ST, p=P)

        @block.sync
        def _(sp):
            def load(q, k):
                wait(sp, placed, q - 3)
                sp.dma_start(zs[:, k].rearrange("p (a s) d -> p a s d", a=1),
                             zs_v[bass.ds(q, 1)].rearrange("a p s d -> p a s d")).then_inc(zs_in[k], 16)

            over_tiles(sp, load)

        @block.gpsimd
        def _(pool):
            def send(q, k):
                pool.wait_ge(ye_r, q + 1)
                pool.sem_inc(ye_seen, 1)
                for s in range(ST):
                    nc.gpsimd.indirect_dma_start(
                        out=ys_dram[:, :],
                        out_offset=bass.IndirectOffsetOnAxis(ap=place[:, k, s:s + 1], axis=0),
                        in_=ye[:, k % 2, s, :], in_offset=None, bounds_check=2 * NTILES * P - 1, oob_is_err=False)\
                        .then_inc(ys_out[k], 16)

            over_tiles(pool, send)
            for s in ys_out:
                pool.wait_ge(s, 16 * ST * QT // 4)

        @block.scalar
        def _(act):
            def norm(q, k):
                par = k % 2
                act.wait_ge(turned, q + 1)
                wait(act, xe_tail, q - 1)
                for c in range(KC):
                    nc.scalar.activation(xe[:, par, c], turn_bank[par][:, c], ACT.Identity, bias=beta[:, c:c + 1],
                                         scale=gamma[:, c:c + 1]).then_inc(xe_r, 1)

            def gelus(q, k):
                par = k % 2
                e = act.value_load(tile_expert[0:1, bass.ds(q, 1)], min_val=0, max_val=NE - 1)
                for c in range(FC):
                    if c % 2 == 0:
                        act.wait_ge(up_done, 2 * q + c // 2 + 1)
                        wait(act, h_tail, 2 * (q - 1))
                    nc.scalar.activation(hf[:, par, c], up_bank[par][c // 2][:, c % 2], ACT.Gelu,
                                         bias=eb1[:, bass.ds(e * FC + c, 1)]).then_inc(hf_r, 1)

            def results(q, k):
                par = k % 2
                act.wait_ge(down_done, q + 1)
                if not (isinstance(q, int) and q < 2):
                    before = (k - 2) % 4
                    act.wait_ge(ys_out[before], (q - 2 - before) * 4 * ST + 16 * ST)
                nc.scalar.activation(ye[:, par], down_bank[par][:, :, :], ACT.Copy).then_inc(ye_r, 1)

            def body(q, k):
                norm(q + 1, (k + 1) % 4)
                gelus(q, k)
                if not (isinstance(q, int) and q == 0):
                    results(q - 1, (k - 1) % 4)

            norm(0, 0)
            over_tiles(act, body, last=QT - 1)
            gelus(QT - 1, 3)
            results(QT - 2, 2)
            results(QT - 1, 3)

        @block.vector
        def _(dve):
            def split(q, k):
                par = k % 2
                dve.wait_ge(xe_r, KC * q + KC)
                wait(dve, up_done, 2 * (q - 1))
                nc.vector.tensor_copy(xe_s[:, par, 0], xe[:, par]).then_inc(xe_head, 1)
                wait(dve, ys_out[k], (q - k) * 4 * ST)
                nc.vector.tensor_copy(place[:, k], zs[:, k, :, D].bitcast(U32)).then_inc(placed, 1)
                dve.wait_ge(xe_head, q + 1)
                nc.vector.tensor_tensor(xe_s[:, par, 1], xe[:, par], xe_s[:, par, 0], ALU.subtract)\
                    .then_inc(xe_tail, 1)

            def split_hidden(q, k):
                par = k % 2
                wait(dve, down_done, q - 1)
                for c in range(0, FC, 2):
                    dve.wait_ge(hf_r, FC * q + c + 2)
                    nc.vector.tensor_copy(h_s[:, par, 0, c:c + 2], hf[:, par, c:c + 2]).then_inc(h_head, 1)
                for c in range(0, FC, 2):
                    dve.wait_ge(h_head, FC // 2 * q + c // 2 + 1)
                    nc.vector.tensor_tensor(h_s[:, par, 1, c:c + 2], hf[:, par, c:c + 2], h_s[:, par, 0, c:c + 2],
                                            ALU.subtract).then_inc(h_tail, 1)

            def body(q, k):
                split(q + 1, (k + 1) % 4)
                split_hidden(q, k)

            split(0, 0)
            over_tiles(dve, body, last=QT - 1)
            split_hidden(QT - 1, 3)

        @block.tensor
        def _(pe):
            def turn(q, r):
                par = r % 2
                pe.wait_ge(zs_in[r], (q - r) * 4 + 16)
                wait(pe, xe_r, KC * (q - 1))
                for c in range(KC):
                    for s in range(ST):
                        last = nc.tensor.transpose(turn_bank[par][:, c, s * P:(s + 1) * P],
                                                   zs[:, r, s, c * P:(c + 1) * P], ident[:, :])
                last.then_inc(turned, 1)

            def up(q, r, e):
                par = r % 2
                pe.wait_ge(xe_tail, q + 1)
                for c in range(FC):
                    if c % 2 == 0:
                        wait(pe, hf_r, FC * (q - 2) + c + 2)
                    last = split_product(nc, up_bank[par][c // 2][:, c % 2],
                                         lambda s, k: w1_s[:, s, bass.ds(e * (KC * FE) + (k * FE + c * P), P)],
                                         lambda s, k: xe_s[:, par, s, k], KC)
                    if c % 2:
                        last.then_inc(up_done, 1)

            def down(q, r, e):
                par = r % 2
                pe.wait_ge(h_tail, 2 * q + 2)
                wait(pe, ye_r, q - 1)
                for n in range(ST):
                    last = split_product(nc, down_bank[par][:, n], lambda s, k: h_s[:, par, s, k, n * P:(n + 1) * P],
                                         lambda s, k: w2_s[:, s, bass.ds(e * (FC * D) + k * D, D)], FC)
                last.then_inc(down_done, 1)

            def expert_of(q):
                return pe.value_load(tile_expert[0:1, bass.ds(q, 1)], min_val=0, max_val=NE - 1)

            def body(q, k):
                turn(q + 1, (k + 1) % 4)
                up(q, k, expert_of(q))
                if not (isinstance(q, int) and q == 0):
                    down(q - 1, (k - 1) % 4, expert_of(q - 1))

            turn(0, 0)
            over_tiles(pe, body, last=QT - 1)
            up(QT - 1, 3, expert_of(QT - 1))
            down(QT - 2, 2, expert_of(QT - 2))
            down(QT - 1, 3, expert_of(QT - 1))


def combine(nc, kept, ab_dram, abx_dram, ys_dram, out):
    ident, eb2r, gc2_row, gc_b, neg_half, eps_t, wdense, wtop, gate_part = [kept[n] for n in (
        "ident", "eb2r", "gc2_row", "gc_b", "neg_half", "eps_t", "wdense", "wtop", "gate_part")]
    IN, MIX = 4, 3
    ctx = ExitStack()
    with ctx:
        def sb(name, shape, dt=F32):
            return ctx.enter_context(nc.sbuf_tensor(name, shape, dt))

        def pb(name, shape, dt=F32):
            return ctx.enter_context(nc.psum_tensor(name, shape, dt))

        def sem(name):
            return ctx.enter_context(nc.semaphore(name))

        bias_bank = [[pb(f"cbias{k}{h}", [P, 2, D]) for h in range(2)] for k in range(2)]
        wdT_bank = [pb(f"cwdT{k}", [P, 512]) for k in range(2)]
        got = sb("got", [P, IN, 2, TT, D])
        abel = sb("abel_c", [P, IN, TT, D])
        abx = sb("abx_c", [P, IN, TT, D])
        wdT = sb("wdT", [NE, BATCHES, TT, P])
        moe = sb("moe", [P, MIX, TT, D])
        diff = sb("diff", [P, 2, TT, D])
        scrap = sb("scrap_c", [P, TT, D])
        s2, gate = sb("s2", [P, 2, TT]), sb("gate_c", [P, 2, TT])
        st, mv, rs = sb("st_c", [P, TT, 6]), sb("mv_c", [P, 2, TT, 2]), sb("rs_c", [P, 2, TT])
        shift = sb("shift", [P, 2, TT])
        res = sb("res", [P, 2, TT, D])
        rows_in = [sem(f"c_rows_in{k}") for k in range(IN)]
        out_stored = [sem("c_stored0"), sem("c_stored1")]
        (wdT_done, wdT_r, bias_done, first_r, moe_r, part_r, sum_r, diff_r, gate_r, mix_r, st_r, mv_r, ve_r, rs_r,
         shift_r, res_r) = [
            sem("c_" + n) for n in ("wdT_done", "wdT_r", "bias_done", "first_r", "moe_r", "part_r", "sum_r", "diff_r",
                                    "gate_r", "mix_r", "st_r", "mv_r", "ve_r", "rs_r", "shift_r", "res_r")]
        block = ctx.enter_context(nc.Block())

        def rows_of(dram, b):
            return dram[b].rearrange("(t p) d -> p t d", p=P)

        ys_v = ys_dram.rearrange("(r b t p) d -> r b p t d", r=2, b=BATCHES, p=P)

        @block.sync
        def _(sp):
            def load(b):
                wait(sp, mix_r, TT * (b - IN + 1))
                for r in range(2):
                    sp.dma_start(got[:, b % IN, r], ys_v[r, b]).then_inc(rows_in[b % IN], 16)
                sp.dma_start(abel[:, b % IN], rows_of(ab_dram, b)).then_inc(rows_in[b % IN], 16)
                sp.dma_start(abx[:, b % IN], rows_of(abx_dram, b)).then_inc(rows_in[b % IN], 16)

            def store(b):
                sp.wait_ge(res_r, TT * (b + 1))
                sp.dma_start(rows_of(out, b), res[:, b % 2]).then_inc(out_stored[b % 2], 16)

            for b in range(IN):
                load(b)
            for b in range(BATCHES):
                if b + IN < BATCHES:
                    load(b + IN)
                store(b)
            for s in out_stored:
                sp.wait_ge(s, 16 * BATCHES // 2)

        @block.gpsimd
        def _(pool):
            def rstd(b):
                pool.wait_ge(mv_r, TT * b + TT)
                wait(pool, res_r, TT * (b - 1))
                nc.gpsimd.tensor_tensor(rs[:, b % 2], mv[:, b % 2, :, 1], eps_t[:, :], ALU.add).then_inc(ve_r, 1)
                pool.wait_ge(ve_r, b + 1)
                nc.gpsimd.tensor_tensor(rs[:, b % 2], rs[:, b % 2], neg_half[:, :], ALU.pow).then_inc(rs_r, 1)

            def differ(b):
                pool.wait_ge(moe_r, TT * (b + 1))
                wait(pool, mix_r, TT * (b - 1))
                nc.gpsimd.tensor_tensor(diff[:, b % 2], moe[:, b % MIX], abel[:, b % IN], ALU.subtract)\
                    .then_inc(diff_r, 1)

            differ(0)
            differ(1)
            for b in range(BATCHES):
                rstd(b)
                if b + 2 < BATCHES:
                    differ(b + 2)

        @block.scalar
        def _(act):
            def weights(b):
                act.wait_ge(wdT_done, b + 1)
                nc.scalar.activation(wdT[:, b].rearrange("e t p -> e (t p)"), wdT_bank[b % 2][0:NE, :], ACT.Copy)\
                    .then_inc(wdT_r, 1)

            def gates(b):
                act.wait_ge(sum_r, b + 1)
                nc.scalar.activation(gate[:, b % 2], s2[:, b % 2], ACT.Sigmoid, bias=gc_b[:, :]).then_inc(gate_r, 1)

            def results(b):
                act.wait_ge(shift_r, b + 1)
                wait(act, out_stored[b % 2], 16 * (b // 2))
                for n in range(TT):
                    nc.scalar.activation(res[:, b % 2, n], moe[:, b % MIX, n], ACT.Identity,
                                         bias=shift[:, b % 2, n:n + 1], scale=rs[:, b % 2, n:n + 1]).then_inc(res_r, 1)

            for b in range(4):
                weights(b)
            gates(0)
            gates(1)
            for b in range(BATCHES):
                if b + 2 < BATCHES:
                    gates(b + 2)
                if b + 4 < BATCHES:
                    weights(b + 4)
                results(b)

        @block.tensor
        def _(pe):
            def turn(b):
                wait(pe, wdT_r, b - 1)
                for n in range(TT):
                    last = nc.tensor.transpose(wdT_bank[b % 2][0:NE, n * P:(n + 1) * P], wdense[:, b * TT + n, :],
                                               ident[:, :])
                last.then_inc(wdT_done, 1)

            turn(0)
            for b in range(BATCHES):
                if b + 1 < BATCHES:
                    turn(b + 1)
                pe.wait_ge(wdT_r, b + 1)
                wait(pe, first_r, TT * (b - 1))
                for n in range(TT):
                    last = nc.tensor.matmul(bias_bank[b % 2][n // 2][:, n % 2], wdT[:, b, n], eb2r[:, :],
                                            start=True, stop=True)
                last.then_inc(bias_done, 1)

        @block.vector
        def _(dve):
            def weighted(b):
                par = b % 2
                dve.wait_ge(bias_done, b + 1)
                dve.wait_ge(rows_in[b % IN], 64 * (b // IN + 1))
                wait(dve, res_r, TT * (b - MIX + 1))
                for n in range(TT):
                    nc.vector.scalar_tensor_tensor(moe[:, b % MIX, n], got[:, b % IN, 0, n],
                                                   wtop[:, 0, b * TT + n:b * TT + n + 1],
                                                   bias_bank[par][n // 2][:, n % 2], ALU.mult, ALU.add)\
                        .then_inc(first_r, 1)
                for n in range(TT):
                    dve.wait_ge(first_r, TT * b + n + 1)
                    nc.vector.scalar_tensor_tensor(moe[:, b % MIX, n], got[:, b % IN, 1, n],
                                                   wtop[:, 1, b * TT + n:b * TT + n + 1],
                                                   moe[:, b % MIX, n], ALU.mult, ALU.add).then_inc(moe_r, 1)
                wait(dve, gate_r, b - 1)
                wait(dve, part_r, TT * b)
                for n in range(TT):
                    dve.wait_ge(moe_r, TT * b + n + 1)
                    nc.vector.scalar_tensor_tensor(scrap[:, n], moe[:, b % MIX, n], 1.0, gc2_row[:, :],
                                                   ALU.mult, ALU.mult, accum_out=s2[:, par, n:n + 1])\
                        .then_inc(part_r, 1)
                dve.wait_ge(part_r, TT * (b + 1))
                nc.vector.tensor_tensor(s2[:, par], s2[:, par], gate_part[:, b * TT:(b + 1) * TT], ALU.add)\
                    .then_inc(sum_r, 1)

            def mixed(b):
                par = b % 2
                dve.wait_ge(gate_r, b + 1)
                dve.wait_ge(diff_r, b + 1)
                for n in range(TT):
                    nc.vector.scalar_tensor_tensor(moe[:, b % MIX, n], diff[:, par, n], gate[:, par, n:n + 1],
                                                   abx[:, b % IN, n], ALU.mult, ALU.add).then_inc(mix_r, 1)
                for n in range(TT):
                    dve.wait_ge(mix_r, TT * b + n + 1)
                    nc.vector.bn_stats(st[:, n], moe[:, b % MIX, n]).then_inc(st_r, 1)
                wait(dve, shift_r, b - 1)
                for n in range(TT):
                    dve.wait_ge(st_r, TT * b + n + 1)
                    nc.vector.bn_aggr(mv[:, par, n], st[:, n]).then_inc(mv_r, 1)

            def shifts(b):
                par = b % 2
                dve.wait_ge(rs_r, b + 1)
                nc.vector.scalar_tensor_tensor(shift[:, par], mv[:, par, :, 0], -1.0, rs[:, par], ALU.mult, ALU.mult)\
                    .then_inc(shift_r, 1)

            weighted(0)
            weighted(1)
            for b in range(BATCHES):
                mixed(b)
                if b + 2 < BATCHES:
                    weighted(b + 2)
                shifts(b)

def build(nc, t, out, scratch):
    mamba_half(nc, t, scratch["xp"], scratch["zs"])
    moe_half(nc, t, scratch["xp"], scratch["abel"], scratch["abx"], scratch["zs"], scratch["ys"], out)


def kernel(**inputs):
    import numpy as _np
    import concourse.bacc as _bacc
    from concourse import mybir as _mybir
    from concourse.bass_utils import run_bass_kernel_spmd as _run

    a = {k: _np.ascontiguousarray(v) for k, v in inputs.items()}

    def columns(x):
        return x.reshape(-1, P).T

    def rows(x):
        return _np.broadcast_to(x.reshape(1, -1), (P, x.size))

    L, F = "L0_attn_", "L0_ffn_"
    laid = {
        "x": a[L + "x"], "n1w": columns(a[L + "norm1_w"]), "n1b": columns(a[L + "norm1_b"]),
        "n2w": columns(a[L + "norm2_w"]), "n2b": columns(a[L + "norm2_b"]),
        "gate_b": columns(a[L + "gate_b"]), "state_b": columns(a[L + "state_b"]),
        "mlp_b1": columns(a[L + "mlp_b1"]), "out_b_row": rows(a[L + "out_b"]),
        "mlp_b2_row": rows(a[L + "mlp_b2"]), "state_b_row": rows(a[L + "state_b"]),
        "gate_w": a[L + "gate_w"], "state_w": a[L + "state_w"], "out_w": a[L + "out_w"],
        "mlp_w1": a[L + "mlp_w1"], "mlp_w2": a[L + "mlp_w2"],
        "gamma": columns(a[F + "ln_gamma"]), "beta": columns(a[F + "ln_beta"]),
        "abel_w": a[F + "abel_w"], "abel_b": rows(a[F + "abel_b"]),
        "mgw": a[F + "moe_gate_w"], "mgb": rows(a[F + "moe_gate_b"]),
        "ew1": a[F + "ew1"], "eb1": columns(a[F + "eb1"]),
        "ew2": a[F + "ew2"], "ew2t": a[F + "ew2"].transpose(0, 2, 1),
        "eb2": a[F + "eb2"], "eb2t": a[F + "eb2"].T, "gens": a[F + "gens"],
        "gc1_row": rows(a[F + "gc_w"][:D]), "gc2_row": rows(a[F + "gc_w"][D:]), "gc_b": rows(a[F + "gc_b"]),
    }
    nc = _bacc.Bacc("TRN2", target_bir_lowering=False, num_devices=1)
    arrays, t = {}, {}
    for name, x in laid.items():
        x = _np.ascontiguousarray(x)
        arrays["in_" + name] = x
        t[name] = nc.dram_tensor("in_" + name, x.shape, _mybir.dt.from_np(x.dtype), kind="ExternalInput").ap()
    out = nc.dram_tensor("out_0", (BATCHES, TOKENS, D), F32, kind="ExternalOutput").ap()
    scratch = {name: nc.dram_tensor("scratch_" + name, shape, F32, kind="Internal").ap() for name, shape in (
        ("xp", (BATCHES, TOKENS, D)), ("abel", (BATCHES, TOKENS, D)),
        ("abx", (BATCHES, TOKENS, D)),
        ("zs", (QT * SLOT, ROW)), ("ys", (2 * NTILES * P, D)))}
    build(nc, t, out, scratch)
    r = _run(nc, [arrays], core_ids=[0])
    return r.results[0]["out_0"]
```
